# Optimizing a Trainium2 kernel written in Bass

```python
import numpy as np
import jax
import jax.numpy as jnp

def _softmax(x, axis=-1):
    return jax.nn.softmax(x, axis=axis)

def _gelu(x):
    return jax.nn.gelu(x, approximate=True)

def _silu(x):
    return jax.nn.silu(x)

def _sigmoid(x):
    return jax.nn.sigmoid(x)

def _layernorm(x, axis=-1, eps=1e-05):
    m = jnp.mean(x, axis=axis, keepdims=True)
    v = jnp.var(x, axis=axis, keepdims=True)
    return (x - m) / jnp.sqrt(v + eps)

def _scatter_add(tgt, idx, src, axis=0):
    return tgt.at[idx].add(src)

def _segment_sum(src, seg, n):
    return jax.ops.segment_sum(src, seg, n)
kernel_name = 'mk_xattn_ffn_d1_seqx_r8_a8bc39'

def setup_inputs(seed: int=0):
    np.random.seed(seed)
    _w = jnp.asarray

    def _rec_inputs():
        import jax
        import jax.numpy as jnp
        _rk = jax.random.key(seed)
        x = 7.22e-05 + 1 * jax.random.normal(jax.random.fold_in(_rk, 1), (8, 128, 256), jnp.float32)
        _lenS = 128 - jax.random.randint(jax.random.fold_in(_rk, 7), (8,), 0, max(1, 128 // 4) + 1, jnp.int32)
        _lenS2 = 128 - jax.random.randint(jax.random.fold_in(_rk, 8), (8,), 0, max(1, 128 // 4) + 1, jnp.int32)
        _ctx_2048P = jax.random.normal(jax.random.fold_in(_rk, 11), (8, 16, 256), jnp.float32)
        _ctx_2048c = jax.random.dirichlet(jax.random.fold_in(_rk, 511), 0.3 * jnp.ones((16,), jnp.float32), (8, 128))
        _ctx_2048t = jnp.einsum('bsk,bkd->bsd', _ctx_2048c, _ctx_2048P)
        _ctx_2048t = _ctx_2048t * jax.lax.rsqrt(jnp.mean(jnp.square(_ctx_2048t)) + 1e-12) * 0.953939
        ctx_2048 = 4.13588e-05 + 0.999923 * (_ctx_2048t + 0.3 * jax.random.normal(jax.random.fold_in(_rk, 611), (8, 128, 256), jnp.float32))
        return (x, ctx_2048)
    x, ctx_2048 = _rec_inputs()

    def _L0_xattn_setup():
        import jax, jax.numpy as jnp
        import numpy as np
        B, S, DIM, HD = (4, 128, 256, 128)
        H = DIM // HD
        GN_EPS = 0.001

        def _decay_masks(n_heads, seq_len):
            gam = 1.0 - 2.0 ** (-5.0 - jnp.arange(n_heads, dtype=jnp.float32))
            idx = jnp.arange(seq_len, dtype=jnp.float32)
            expo = idx[None, :] - idx[:, None]
            D = jnp.where(expo[None, :, :] <= 0, gam[:, None, None] ** expo[None, :, :], 0.0)
            return D / jnp.sqrt(D.sum(axis=-1))[:, None, :]
        key = jax.random.key(seed)
        ks = jax.random.split(key, 8)
        x = jax.random.normal(ks[0], (B, S, DIM), dtype=jnp.float32)
        k = jax.random.normal(ks[1], (B, S, DIM), dtype=jnp.float32)
        v = jax.random.normal(ks[2], (B, S, DIM), dtype=jnp.float32)
        Wh = jax.random.normal(ks[3], (H, HD, HD), dtype=jnp.float32) / np.sqrt(HD)
        wg_w = jax.random.normal(ks[4], (DIM, DIM), dtype=jnp.float32) / np.sqrt(DIM)
        wo_w = jax.random.normal(ks[5], (DIM, DIM), dtype=jnp.float32) / np.sqrt(DIM)
        gn_gamma = jnp.ones((DIM,), dtype=jnp.float32)
        gn_beta = jnp.zeros((DIM,), dtype=jnp.float32)
        return {'x': x, 'k': k, 'v': v, 'Wh': Wh, 'wg_w': wg_w, 'wo_w': wo_w, 'gn_gamma': gn_gamma, 'gn_beta': gn_beta}
    _L0_xattn_all = _L0_xattn_setup()
    _L0_xattn_in = {k: v for k, v in _L0_xattn_all.items() if k in ('Wh', 'wg_w', 'wo_w', 'gn_gamma', 'gn_beta')}
    del _L0_xattn_all

    def _L0_ffn_setup():
        import jax, jax.numpy as jnp
        import numpy as np
        HIDDEN = 256
        FFN = 176
        N_EXPERTS = 64
        TOP_K = 6
        N_SHARED = 2
        SHARED_FFN = FFN * N_SHARED
        ROUTED_SCALING = 1.0
        EPS = 1e-20

        def _moe_forward(x, gate_w, w_gate_up, w_down, ws_gate_up, ws_down):
            T = x.shape[0]
            logits = jnp.einsum('th,eh->te', x.astype(jnp.float32), gate_w.astype(jnp.float32))
            scores = jax.nn.softmax(logits, axis=-1)
            topk_w, topk_ids = jax.lax.top_k(scores, TOP_K)
            topk_w = topk_w / (jnp.sum(topk_w, axis=-1, keepdims=True) + EPS)
            topk_w = topk_w * ROUTED_SCALING
            comb = jnp.zeros((T, N_EXPERTS), dtype=x.dtype)
            comb = comb.at[jnp.arange(T)[:, None], topk_ids].add(topk_w.astype(x.dtype))
            gu = jnp.einsum('th,efh->tef', x, w_gate_up)
            g, u = (gu[..., :FFN], gu[..., FFN:])
            act = jax.nn.silu(g) * u
            act = act * comb[:, :, None]
            routed = jnp.einsum('tef,ehf->th', act, w_down)
            sgu = jnp.einsum('th,fh->tf', x, ws_gate_up)
            sg, su = (sgu[..., :SHARED_FFN], sgu[..., SHARED_FFN:])
            shared = jnp.einsum('tf,hf->th', jax.nn.silu(sg) * su, ws_down)
            return routed + shared
        key = jax.random.key(seed)
        k0, k1, k2, k3, k4, k5 = jax.random.split(key, 6)
        hidden_states = jax.random.normal(k0, (1, 32, HIDDEN), dtype=jnp.float32)
        gate_w = jax.random.normal(k1, (N_EXPERTS, HIDDEN), dtype=jnp.float32) * 0.05
        w_gate_up = jax.random.normal(k2, (N_EXPERTS, 2 * FFN, HIDDEN), dtype=jnp.float32) * 0.02
        w_down = jax.random.normal(k3, (N_EXPERTS, HIDDEN, FFN), dtype=jnp.float32) * 0.02
        ws_gate_up = jax.random.normal(k4, (2 * SHARED_FFN, HIDDEN), dtype=jnp.float32) * 0.02
        ws_down = jax.random.normal(k5, (HIDDEN, SHARED_FFN), dtype=jnp.float32) * 0.02
        return {'hidden_states': hidden_states, 'gate_w': gate_w, 'w_gate_up': w_gate_up, 'w_down': w_down, 'ws_gate_up': ws_gate_up, 'ws_down': ws_down}
    _L0_ffn_all = _L0_ffn_setup()
    _L0_ffn_in = {k: v for k, v in _L0_ffn_all.items() if k in ('gate_w', 'w_gate_up', 'w_down', 'ws_gate_up', 'ws_down')}
    del _L0_ffn_all
    return {'x': x, 'ctx_2048': ctx_2048, 'L0_xattn_Wh': _L0_xattn_in['Wh'], 'L0_xattn_wg_w': _L0_xattn_in['wg_w'], 'L0_xattn_wo_w': _L0_xattn_in['wo_w'], 'L0_xattn_gn_gamma': _L0_xattn_in['gn_gamma'], 'L0_xattn_gn_beta': _L0_xattn_in['gn_beta'], 'L0_ffn_gate_w': _L0_ffn_in['gate_w'], 'L0_ffn_w_gate_up': _L0_ffn_in['w_gate_up'], 'L0_ffn_w_down': _L0_ffn_in['w_down'], 'L0_ffn_ws_gate_up': _L0_ffn_in['ws_gate_up'], 'L0_ffn_ws_down': _L0_ffn_in['ws_down']}

def reference(x, ctx_2048, L0_xattn_Wh, L0_xattn_wg_w, L0_xattn_wo_w, L0_xattn_gn_gamma, L0_xattn_gn_beta, L0_ffn_gate_w, L0_ffn_w_gate_up, L0_ffn_w_down, L0_ffn_ws_gate_up, L0_ffn_ws_down):
    import jax
    import jax.numpy as jnp

    def _L0_xattn_ref(x, k, v, Wh, wg_w, wo_w, gn_gamma, gn_beta):
        import jax, jax.numpy as jnp
        import numpy as np
        B, S, DIM, HD = (4, 128, 256, 128)
        H = DIM // HD
        GN_EPS = 0.001

        def _decay_masks(n_heads, seq_len):
            gam = 1.0 - 2.0 ** (-5.0 - jnp.arange(n_heads, dtype=jnp.float32))
            idx = jnp.arange(seq_len, dtype=jnp.float32)
            expo = idx[None, :] - idx[:, None]
            D = jnp.where(expo[None, :, :] <= 0, gam[:, None, None] ** expo[None, :, :], 0.0)
            return D / jnp.sqrt(D.sum(axis=-1))[:, None, :]
        b, s, dim = x.shape
        h, hd, _ = Wh.shape
        xh = x.reshape(b, s, h, hd)
        kh = k.reshape(b, s, h, hd)
        vh = v.reshape(b, s, h, hd)
        Q = jnp.einsum('bshd,hde->bshe', xh, Wh)
        K = jnp.einsum('bshd,hde->bshe', kh, Wh)
        V = jnp.einsum('bshd,hde->bshe', vh, Wh)
        scores = jnp.einsum('bshe,bthe->bhst', Q, K) / jnp.sqrt(jnp.float32(hd))
        Dn = _decay_masks(h, s)
        masked = scores * Dn[None, :, :, :]
        A = jnp.maximum(jnp.abs(masked.sum(axis=0)), 1.0)
        O = jnp.einsum('hst,bthe->bshe', A, V).reshape(b, s, dim)
        mu = O.mean(axis=-1, keepdims=True)
        var = O.var(axis=-1, keepdims=True)
        Y = (O - mu) / jnp.sqrt(var + GN_EPS) * gn_gamma + gn_beta
        W = jax.nn.relu(x @ wg_w)
        return W * Y @ wo_w

    def _L0_ffn_ref(hidden_states, gate_w, w_gate_up, w_down, ws_gate_up, ws_down):
        import jax, jax.numpy as jnp
        import numpy as np
        HIDDEN = 256
        FFN = 176
        N_EXPERTS = 64
        TOP_K = 6
        N_SHARED = 2
        SHARED_FFN = FFN * N_SHARED
        ROUTED_SCALING = 1.0
        EPS = 1e-20

        def _moe_forward(x, gate_w, w_gate_up, w_down, ws_gate_up, ws_down):
            T = x.shape[0]
            logits = jnp.einsum('th,eh->te', x.astype(jnp.float32), gate_w.astype(jnp.float32))
            scores = jax.nn.softmax(logits, axis=-1)
            topk_w, topk_ids = jax.lax.top_k(scores, TOP_K)
            topk_w = topk_w / (jnp.sum(topk_w, axis=-1, keepdims=True) + EPS)
            topk_w = topk_w * ROUTED_SCALING
            comb = jnp.zeros((T, N_EXPERTS), dtype=x.dtype)
            comb = comb.at[jnp.arange(T)[:, None], topk_ids].add(topk_w.astype(x.dtype))
            gu = jnp.einsum('th,efh->tef', x, w_gate_up)
            g, u = (gu[..., :FFN], gu[..., FFN:])
            act = jax.nn.silu(g) * u
            act = act * comb[:, :, None]
            routed = jnp.einsum('tef,ehf->th', act, w_down)
            sgu = jnp.einsum('th,fh->tf', x, ws_gate_up)
            sg, su = (sgu[..., :SHARED_FFN], sgu[..., SHARED_FFN:])
            shared = jnp.einsum('tf,hf->th', jax.nn.silu(sg) * su, ws_down)
            return routed + shared
        B, S, H = hidden_states.shape
        x = hidden_states.reshape(-1, H)
        out = _moe_forward(x, gate_w, w_gate_up, w_down, ws_gate_up, ws_down)
        return out.reshape(B, S, H)
    x = x + _L0_xattn_ref(_layernorm(x, axis=-1), ctx_2048, ctx_2048, L0_xattn_Wh, L0_xattn_wg_w, L0_xattn_wo_w, L0_xattn_gn_gamma, L0_xattn_gn_beta)
    x = x + _L0_ffn_ref(_layernorm(x, axis=-1), L0_ffn_gate_w, L0_ffn_w_gate_up, L0_ffn_w_down, L0_ffn_ws_gate_up, L0_ffn_ws_down)
    return x

_drawn_inputs = setup_inputs


def setup_inputs(seed=0):
    import zlib

    import numpy as np

    out = dict(_drawn_inputs(seed))
    spreads = {'L0_xattn_gn_gamma': (1.0, 0.2), 'L0_xattn_gn_beta': (0.0, 0.1)}
    factors = {'L0_ffn_gate_w': 8.0,
     'L0_ffn_w_gate_up': 8.0,
     'L0_ffn_w_down': 8.0,
     'L0_ffn_ws_gate_up': 3.539,
     'L0_ffn_ws_down': 3.539}
    for name, (base, spread) in spreads.items():
        noise = np.random.default_rng([zlib.crc32(name.encode()), seed]).standard_normal(out[name].shape)
        drawn = base * np.exp(spread * noise) if base else spread * noise
        out[name] = jnp.asarray(drawn.astype(out[name].dtype))
    for name, factor in factors.items():
        out[name] = (out[name] * factor).astype(out[name].dtype)
    return out
```

```python
import numpy as np
import concourse.bass as bass
from concourse import mybir
from contextlib import ExitStack

B, S, D = 8, 128, 256
N = B * S
H, HD = 2, 128
KD = D // 128
E, F, TOPK = 64, 176, 6
SF = 2 * F
FC = 88
LN_EPS, GN_EPS, TOP_EPS = 1e-5, 1e-3, 1e-20
MAXE = N // 128
BLK = MAXE + 1
COLS = (MAXE - 1) * E
EXTRA = (N * TOPK) // 128
TILES = E + EXTRA
R = 16
U = 8
LOOK_ID, LOOK_G = 5, 4
HALF = 4 * S


def program(nc, x, ctxT, Wh, wg, wo, gam, bet, gw, wgu, wdn, wsg, wsd, cst, out):
    f32, i32, u32 = mybir.dt.float32, mybir.dt.int32, mybir.dt.uint32
    ALU, ACT, AX = mybir.AluOpType, mybir.ActivationFunctionType, mybir.AxisListType

    tbl = nc.dram_tensor("slot_table", [BLK * 128, E, 2], i32).ap()
    hbuf = nc.dram_tensor("h_rows", [N + 128, D], f32).ap()
    acc1 = nc.dram_tensor("acc_odd", [N + 128, D], f32).ap()
    lst_d = nc.dram_tensor("tile_list", [128, 2], i32).ap()

    with ExitStack() as ctx:
        def sb(name, shape, dt=f32):
            return ctx.enter_context(nc.sbuf_tensor(name, shape, dt))

        def sem(name):
            return ctx.enter_context(nc.semaphore(name))

        X = sb("X", [128, B, D])
        CT = sb("CT", [128, H, N])
        XN = sb("XN", [128, B, D])
        XNT = sb("XNT", [128, KD, N])
        QT = sb("QT", [128, H, N])
        KT = sb("KT", [128, H, N])
        V = sb("V", [128, H, B, HD])
        HT, WR = CT, XN
        YN = KT[:, :, :].rearrange("p h n -> p (h n)").rearrange("p (b d) -> p b d", b=B)
        HN = QT[:, :, :].rearrange("p h n -> p (h n)").rearrange("p (b d) -> p b d", b=B)
        WH = sb("WH", [128, H, HD])
        WGT = sb("WGT", [128, KD, D])
        WOT = sb("WOT", [128, KD, D])
        GWT = sb("GWT", [128, KD, E])
        WSG = sb("WSG", [128, KD, 2 * SF])
        WSD = sb("WSD", [FC, SF // FC, D])
        GAM = sb("GAM", [128, D])
        BET = sb("BET", [128, D])
        CST = sb("CST", [128, 512])
        IDN, TRI, MASK = CST[:, 0:128], CST[:, 128:256], CST[:, 256:512]
        ONE = sb("ONE", [128, 128])
        IOE = sb("IOE", [128, E])
        THR = sb("THR", [128, COLS])
        PM64 = sb("PM64", [128, 1])
        PMIN = sb("PMIN", [128, 1])
        ZERO = sb("ZERO", [128, 512])
        INIT = sb("INIT", [128, E, 2], i32)
        PAY = sb("PAY", [128, B, TOPK, 2], i32)
        SLOT = sb("SLOT", [128, B, TOPK], i32)
        AT = sb("AT", [128, H, S])
        AT0 = sb("AT0", [128, H, S])
        AT1 = sb("AT1", [128, H, S])
        NHALF = sb("NHALF", [128, 1])
        ST1 = sb("ST1", [128, B, 6])
        MV1 = sb("MV1", [128, B, 2])
        RS1 = sb("RS1", [128, B])
        STG = sb("STG", [128, B, 6])
        MVG = sb("MVG", [128, B, 2])
        VE1 = sb("VE1", [128, B])
        VEG = sb("VEG", [128, B])
        VE2 = sb("VE2", [128, 1])
        RSG = sb("RSG", [128, B])
        NBG = sb("NBG", [128, B])
        ST2 = sb("ST2", [128, 6])
        MV2 = sb("MV2", [128, 2])
        RS2 = sb("RS2", [128, 1])
        Y0 = sb("Y0", [128, D])
        Y1 = sb("Y1", [128, D])
        Z = sb("Z", [128, 2, D])
        ZT = sb("ZT", [128, 2, KD, 128])
        NM = sb("NM", [128, 1])
        EX = sb("EX", [128, E])
        ZS = sb("ZS", [128, 1])
        SC = sb("SC", [128, E])
        TOP = sb("TOP", [128, 8])
        IDX = sb("IDX", [128, 8], u32)
        IDF = sb("IDF", [128, 2, 8])
        TS = sb("TS", [128, 1])
        RT = sb("RT", [128, 1])
        RZ = sb("RZ", [128, 1])
        OH = sb("OH", [128, 2, TOPK, E])
        SEL = sb("SEL", [128, TOPK, E])
        RK = sb("RK", [128, TOPK])
        M = sb("M", [128, 2, E])
        MS = sb("MS", [128, B + 1, E])
        SEX = sb("SEX", [128, SF])
        SSG = sb("SSG", [128, SF])
        SRC = sb("SRC", [128, SF])
        SAC = sb("SAC", [128, SF])
        SACT = sb("SACT", [FC, SF // FC, 128])
        OVF = sb("OVF", [128, COLS])
        PRE = sb("PRE", [128, COLS])
        LE = sb("LE", [128, COLS])
        CNT = sb("CNT", [128, 1])
        LST = sb("LST", [128, 2], i32)
        TT = sb("TT", [1, 1], i32)
        LROW = sb("LROW", [1, 256], i32)
        TBL = sb("TBL", [128, BLK * E * 2], i32)
        IDR = sb("IDR", [128, U, 2], i32)
        XG = sb("XG", [128, LOOK_G, D])
        XT = sb("XT", [128, 2, KD, 128])
        SG = sb("SG", [128, 2, F])
        AC = sb("AC", [128, 2, F])
        ATT = sb("ATT", [FC, 2, 2, 128])
        YS = sb("YS", [128, 4, D])
        WGU = sb("WGU", [128, R * 2 * SF])
        WDN = sb("WDN", [FC, R * 2 * D])
        RANK, ZTB, WO, HTB, LOGIT, GATE, UP, SDB = range(8)
        PS = ctx.enter_context(nc.psum_tensor("PS", [128, 8, 512], f32))

        ld = {n: sem("ld_" + n) for n in ("ctx", "wh", "x", "cst", "wg", "wo", "gb", "gw", "wsg", "wsd")}
        s_const, s_init = sem("s_const"), sem("s_init")
        s_kt, s_ktc, s_v, s_vc, s_xn, s_xt, s_xtc, s_q, s_qc = (
            sem(n) for n in ("s_kt", "s_ktc", "s_v", "s_vc", "s_xn", "s_xt", "s_xtc", "s_q", "s_qc"))
        s_sc, s_a, s_wr, s_wrc, s_o = (sem(n) for n in ("s_sc", "s_a", "s_wr", "s_wrc", "s_o"))
        s_z, s_zt, s_ztc, s_wo, s_x2, s_h, s_ht, s_htc = (
            sem(n) for n in ("s_z", "s_zt", "s_ztc", "s_wo", "s_x2", "s_h", "s_ht", "s_htc"))
        s_lg, s_nm, s_ex, s_m, s_rk, s_slot = (sem(n) for n in ("s_lg", "s_nm", "s_ex", "s_m", "s_rk", "s_slot"))
        s_sgu, s_sex, s_sact, s_st, s_stc, s_sd, s_xs = (
            sem(n) for n in ("s_sgu", "s_sex", "s_sact", "s_st", "s_stc", "s_sd", "s_xs"))
        s_v1, s_r1, s_vg, s_rg, s_nb, s_yn, s_v2, s_r2 = (
            sem(n) for n in ("s_v1", "s_r1", "s_vg", "s_rg", "s_nb", "s_yn", "s_v2", "s_r2"))
        s_cnt, s_list, s_lstd, s_lrow = sem("s_cnt"), sem("s_list"), sem("s_lstd"), sem("s_lrow")
        s_tsc, s_tbl, s_hst, s_ost = sem("s_tsc"), sem("s_tbl"), sem("s_hst"), sem("s_ost")
        s_dve = sem("s_dve")
        s_w = [sem(f"s_w{u}") for u in range(U)]
        s_g = [sem(f"s_g{u}") for u in range(LOOK_G)]
        s_acc = [sem(f"s_acc{u}") for u in range(2)]
        s_id, s_xg, s_xgc, s_gu, s_sg, s_act, s_at, s_atc, s_d, s_y = (
            sem(n) for n in ("m_id", "m_xt", "m_xtc", "m_gu", "m_sg", "m_act", "m_at", "m_atc", "m_d", "m_y"))
        s_fin, s_turn, s_sp = sem("s_fin"), sem("s_turn"), sem("s_sp")

        block = ctx.enter_context(nc.Block())

        def ge(eng, s, v):
            if not isinstance(v, int) or v > 0:
                eng.wait_ge(s, v)

        def heads_of(b):
            return PS[:, 4 + 2 * (b // 4):6 + 2 * (b // 4), (b % 4) * HD:(b % 4 + 1) * HD]

        @block.sync
        def _(sp):
            sp.dma_start(WH[:], Wh).then_inc(ld["wh"], 16)
            sp.dma_start(CT[:], ctxT).then_inc(ld["ctx"], 16)
            sp.dma_start(X[:], x).then_inc(ld["x"], 16)
            sp.dma_start(CST[:], cst).then_inc(ld["cst"], 16)
            sp.dma_start(WGT[:], wg).then_inc(ld["wg"], 16)
            sp.dma_start(WOT[:], wo).then_inc(ld["wo"], 16)
            sp.dma_start(GAM[:], gam).then_inc(ld["gb"], 16)
            sp.dma_start(BET[:], bet).then_inc(ld["gb"], 16)
            sp.dma_start(GWT[:], gw).then_inc(ld["gw"], 16)
            sp.dma_start(WSG[:], wsg).then_inc(ld["wsg"], 16)
            sp.dma_start(WSD[:], wsd).then_inc(ld["wsd"], 16)
            sp.wait_ge(s_const, 1)
            blocks = "(k p) e c -> p k (e c)"
            sp.dma_start(tbl.rearrange(blocks, p=128),
                         INIT[:].rearrange("p e c -> p (e c)").unsqueeze(1).to_broadcast([128, BLK, 2 * E])).then_inc(s_init, 16)
            sp.dma_start(acc1.rearrange("(k p) d -> p k d", p=128),
                         ZERO[:, 0:D].unsqueeze(1).to_broadcast([128, N // 128 + 1, D])).then_inc(s_init, 16)
            sp.dma_start(hbuf[N:N + 128, :], ZERO[:, 0:D]).then_inc(s_init, 16)
            sp.dma_start(out[N:N + 128, :], ZERO[:, 0:D]).then_inc(s_init, 16)

            def load(slot, u, e):
                sp.dma_start(WGU[:, slot * 2 * SF:(slot + 1) * 2 * SF], wgu[e]).then_inc(s_w[u], 16)
                sp.dma_start(WDN[:, slot * 2 * D:(slot + 1) * 2 * D], wdn[e]).then_inc(s_w[u], 16)

            def load_dyn(i, u, e):
                slot = (i % 2) * U + u
                sp.dma_start(WGU[:, bass.ds(slot * (2 * SF), 2 * SF)],
                             wgu[bass.ds(e, 1)].rearrange("o p n -> (o p) n")).then_inc(s_w[u], 16)
                sp.dma_start(WDN[:, bass.ds(slot * (2 * D), 2 * D)],
                             wdn[bass.ds(e, 1)].rearrange("o p n -> (o p) n")).then_inc(s_w[u], 16)

            for t in range(R):
                ge(sp, s_w[t % U], 32 * (t // U))
                load(t, t % U, t)
            for b in range(B):
                sp.wait_ge(s_h, b + 1)
                sp.dma_start(hbuf[b * S:(b + 1) * S, :], HN[:, b, :]).then_inc(s_hst, 16)
            sp.wait_ge(s_list, 1)
            sp.dma_start(lst_d, LST[:]).then_inc(s_lstd, 16)
            sp.wait_ge(s_lstd, 16)
            sp.dma_start(LROW[:], lst_d.rearrange("(o t) c -> o (t c)", o=1)).then_inc(s_lrow, 16)
            for b in range(B):
                sp.wait_ge(s_xs, b + 1)
                sp.dma_start(out[b * S:(b + 1) * S, :], X[:, b, :]).then_inc(s_ost, 16)
            T = sp.value_load(TT[0:1, 0:1], min_val=E, max_val=TILES - 1)
            sp.wait_ge(s_lrow, 16)
            with sp.Fori(R // U, E // U) as i:
                for u in range(U):
                    sp.wait_ge(s_d, i * U + (u - R + 1))
                    sp.sem_inc(s_sp)
                    sp.wait_ge(s_w[u], i * 32)
                    sp.sem_inc(s_sp)
                    load_dyn(i, u, i * U + u)
            with sp.Fori(E // U, TILES // U) as i:
                for u in range(U):
                    with sp.If(i * U + (u - 1) < T):
                        e = sp.value_load(LROW[0:1, bass.ds(i * (2 * U) + (2 * u + 1), 1)], min_val=0, max_val=E - 1)
                        sp.wait_ge(s_d, i * U + (u - R + 1))
                        sp.sem_inc(s_sp)
                        sp.wait_ge(s_w[u], i * 32)
                        sp.sem_inc(s_sp)
                        load_dyn(i, u, e)

        @block.gpsimd
        def _(pool):
            nc.gpsimd.memset(INIT[:], 0).then_inc(s_init, 1)
            pool.wait_ge(s_init, 1)
            nc.gpsimd.iota(INIT[:, :, 0], [[0, E]], base=N, channel_multiplier=1)
            nc.gpsimd.memset(ZERO[:], 0.0)
            nc.gpsimd.memset(ONE[:], 1.0)
            nc.gpsimd.memset(MS[:, 0, :], 0.0)
            nc.gpsimd.memset(NHALF[:], -0.5)
            nc.gpsimd.iota(PAY[:, :, :, 0], [[S, B], [0, TOPK]], base=0, channel_multiplier=1)
            nc.gpsimd.iota(IOE[:], [[1, E]], base=0, channel_multiplier=0, allow_small_or_imprecise_dtypes=True)
            nc.gpsimd.iota(THR[:], [[128, MAXE - 1], [0, E]], base=128, channel_multiplier=0,
                           allow_small_or_imprecise_dtypes=True)
            nc.gpsimd.iota(PM64[:], [[0, 1]], base=-E, channel_multiplier=1,
                           allow_small_or_imprecise_dtypes=True).then_inc(s_init, 1)
            pool.wait_ge(s_init, 2)
            nc.gpsimd.tensor_scalar(PMIN[:], PM64[:], float(E), float(E), ALU.add, ALU.min).then_inc(s_const, 1)
            minus_half = NHALF[:, 0:1].to_broadcast([128, B])
            pool.wait_ge(s_v1, 1)
            nc.gpsimd.tensor_tensor(RS1[:], VE1[:], minus_half, ALU.pow).then_inc(s_r1, 1)
            pool.wait_ge(s_vg, 1)
            nc.gpsimd.tensor_tensor(RSG[:], VEG[:], minus_half, ALU.pow).then_inc(s_rg, 1)
            for i in range(B + 2):
                if i < B:
                    pool.wait_ge(s_v2, i + 1)
                    ge(pool, s_h, i)
                    nc.gpsimd.tensor_tensor(RS2[:], VE2[:], NHALF[:], ALU.pow).then_inc(s_r2, 1)
                b = i - 2
                if b < 0:
                    continue
                if b == 0:
                    pool.wait_ge(s_init, 2 + 4 * 16)
                pool.wait_ge(s_slot, b + 1)
                for j in range(TOPK):
                    pool.indirect_dma_start(tbl.rearrange("r e c -> (r e) c"),
                                            bass.IndirectOffsetOnAxis(ap=SLOT[:, b, j:j + 1], axis=0),
                                            PAY[:, b, j, :], None).then_inc(s_tsc, 16)

            def gather(g, idr):
                pool.indirect_dma_start(XG[:, g, :], None, hbuf,
                                        bass.IndirectOffsetOnAxis(ap=IDR[:, idr, 0:1], axis=0)).then_inc(s_g[g], 16)

            def step(i, u):
                t = i * U
                ge(pool, s_id, t + (u + LOOK_G + 1))
                ge(pool, s_xg, t + (u + 1))
                pool.sem_inc(s_turn)
                gather((u + LOOK_G) % LOOK_G, (u + LOOK_G) % U)
                ge(pool, s_y, t + (u + 1))
                ge(pool, s_acc[u % 2], i * (16 * U // 2) + 16 * (u // 2))
                pool.sem_inc(s_turn)
                pool.indirect_dma_start((out, acc1)[u % 2],
                                        bass.IndirectOffsetOnAxis(ap=IDR[:, u, 0:1], axis=0),
                                        YS[:, u % 4, :], None, compute_op=ALU.add).then_inc(s_acc[u % 2], 16)

            pool.wait_ge(s_hst, 16 * B)
            for t in range(LOOK_G):
                ge(pool, s_id, t + 1)
                gather(t, t)
            pool.wait_ge(s_ost, 16 * B)
            T = pool.value_load(TT[0:1, 0:1], min_val=E, max_val=TILES - 1)
            for u in range(U):
                step(0, u)
            with pool.Fori(1, E // U - 1) as i:
                for u in range(U):
                    step(i, u)
            with pool.Fori(E // U - 1, TILES // U) as i:
                for u in range(U):
                    with pool.If(i * U + u < T):
                        step(i, u)
            for g in range(LOOK_G):
                pool.wait_ge(s_g[g], (T + (2 * LOOK_G - 1 - g)) // LOOK_G * 16)
            pool.wait_ge(s_acc[0], (T + 1) // 2 * 16)
            pool.wait_ge(s_acc[1], T // 2 * 16)
            pool.sem_inc(s_turn)
            pool.dma_start(out[0:N, :], acc1[0:N, :], accum_op=ALU.add, max_dma_last_dim=8192).then_inc(s_fin, 16)
            pool.wait_ge(s_fin, 16)

        @block.scalar
        def _(act):
            for j in range(4):
                act.wait_ge(s_kt, j + 1)
                nc.scalar.copy(KT[:, j % 2, (j // 2) * HALF:(j // 2 + 1) * HALF], PS[:, j, :]).then_inc(s_ktc, 1)
            for g in range(4):
                act.wait_ge(s_v, g + 1)
                nc.scalar.copy(V[:, :, 2 * g:2 * g + 2, :],
                               PS[:, 4 + g, :].rearrange("p (h b e) -> p h b e", h=H, b=2)).then_inc(s_vc, 1)
            for j in range(4):
                act.wait_ge(s_q, j + 1)
                nc.scalar.copy(QT[:, j % 2, (j // 2) * HALF:(j // 2 + 1) * HALF], PS[:, 4 + j, :]).then_inc(s_qc, 1)
            for g in range(4):
                act.wait_ge(s_wr, g + 1)
                nc.scalar.activation(WR[:, 2 * g:2 * g + 2, :],
                                     PS[:, 1 + g % 3, :].rearrange("p (b d) -> p b d", b=2), ACT.Relu).then_inc(s_wrc, 1)
            act.wait_ge(s_nb, 1)
            for b in range(B):
                nc.scalar.activation(YN[:, b, :].rearrange("p (h e) -> p h e", h=H), heads_of(b), ACT.Identity,
                                     bias=NBG[:, b:b + 1], scale=RSG[:, b:b + 1]).then_inc(s_yn, 1)
            for i in range(B + 2):
                a, r, s = i, i - 1, i - 2
                if a < B:
                    act.wait_ge(s_zt, a + 1)
                    ge(act, s_wo, a - 1)
                    nc.scalar.copy(ZT[:, a % 2, :, :],
                                   PS[:, ZTB, 0:256].rearrange("p (k n) -> p k n", k=KD)).then_inc(s_ztc, 1)
                if 0 <= s < B:
                    act.wait_ge(s_nm, s + 1)
                    ge(act, s_m, s)
                    nc.scalar.activation(EX[:], PS[:, LOGIT, 0:E], ACT.Exp, bias=NM[:, 0:1],
                                         accum_out=ZS[:, 0:1]).then_inc(s_ex, 1)
                    act.wait_ge(s_sgu, s + 1)
                    ge(act, s_sact, s)
                    nc.scalar.activation(SEX[:], PS[:, GATE, 0:SF], ACT.Exp, scale=-1.0).then_inc(s_sex, 1)
                    act.wait_ge(s_st, s + 1)
                    ge(act, s_sd, s)
                    nc.scalar.copy(SACT[:], PS[0:FC, GATE, :].rearrange("p (c n) -> p c n", c=SF // FC)).then_inc(s_stc, 1)
                if 0 <= r < B:
                    act.wait_ge(s_ht, r + 1)
                    nc.scalar.copy(HT[:, :, r * S:(r + 1) * S],
                                   PS[:, HTB, 0:256].rearrange("p (k n) -> p k n", k=KD)).then_inc(s_htc, 1)
            act.wait_ge(s_tsc, 16 * TOPK * B)
            act.dma_start(TBL[:].rearrange("p (k n) -> p k n", k=BLK),
                          tbl.rearrange("(k p) e c -> p k (e c)", p=128)).then_inc(s_tbl, 16)

            def rows_in(t, v):
                ge(act, s_xg, t + (v + 1))
                ge(act, s_gu, t + (v - 1))
                nc.scalar.copy(XT[:, v % 2, :, :],
                               PS[:, v % 2, 0:256].rearrange("p (k n) -> p k n", k=KD)).then_inc(s_xgc, 1)

            def silu(t, v):
                ge(act, s_gu, t + (v + 1))
                ge(act, s_act, t + (v - 1))
                nc.scalar.activation(SG[:, v % 2, :], PS[:, 2 + v % 2, 0:F], ACT.Silu).then_inc(s_sg, 1)

            def step(i, u):
                t = i * U
                rows_in(t, u + 2)
                silu(t, u + 1)
                ge(act, s_d, t + (u + 1))
                ge(act, s_acc[u % 2], i * (16 * U // 2) + 16 * (u // 2 - 1))
                nc.scalar.copy(YS[:, u % 4, :], PS[:, 6 + u % 2, 0:D]).then_inc(s_y, 1)

            act.wait_ge(s_cnt, 1)
            rows_in(0, 0)
            rows_in(0, 1)
            silu(0, 0)
            act.wait_ge(s_list, 1)
            T = act.value_load(TT[0:1, 0:1], min_val=E, max_val=TILES - 1)
            for u in range(U):
                step(0, u)
            with act.Fori(1, E // U - 1) as i:
                for u in range(U):
                    step(i, u)
            with act.Fori(E // U - 1, TILES // U) as i:
                for u in range(U):
                    with act.If(i * U + u < T):
                        step(i, u)

        @block.vector
        def _(dve):
            count = [0]

            def link(ins):
                count[0] += 1
                ins.then_inc(s_dve, 1)
                dve.wait_ge(s_dve, count[0])

            def mark(ins, s):
                ins.then_inc(s, 1)

            v = nc.vector
            dve.wait_ge(ld["x"], 16)
            for b in range(B):
                last = v.bn_stats(ST1[:, b, :], X[:, b, :])
            link(last)
            for b in range(B):
                last = v.bn_aggr(MV1[:, b, :], ST1[:, b, :])
            link(last)
            v.tensor_scalar(VE1[:], MV1[:, :, 1], LN_EPS, None, ALU.add).then_inc(s_v1, 1)
            dve.wait_ge(s_r1, 1)
            for b in range(B):
                v.tensor_scalar(XN[:, b, :], X[:, b, :], MV1[:, b, 0:1], RS1[:, b:b + 1],
                                ALU.subtract, ALU.mult).then_inc(s_xn, 1)
            for g in range(4):
                dve.wait_ge(s_xt, g + 1)
                v.tensor_copy(XNT[:, :, g * 256:(g + 1) * 256],
                              PS[:, g, :].rearrange("p (k n) -> p k n", k=KD)).then_inc(s_xtc, 1)
            dve.wait_ge(s_sc, 1)
            link(v.scalar_tensor_tensor(AT0[:].rearrange("p h s -> p (h s)"), PS[:, 0, 0:256], float(np.float32(1.0) / np.sqrt(np.float32(HD))),
                                        MASK, ALU.mult, ALU.mult))
            link(v.scalar_tensor_tensor(AT1[:], AT0[:], -1.0, AT0[:], ALU.mult, ALU.max))
            v.tensor_scalar(AT[:], AT1[:], 1.0, None, ALU.max).then_inc(s_a, 1)
            for b in range(B):
                if b % 4 == 0:
                    dve.wait_ge(s_o, b // 4 + 1)
                last = v.bn_stats(STG[:, b, :], heads_of(b))
            link(last)
            for b in range(B):
                last = v.bn_aggr(MVG[:, b, :], STG[:, b, :])
            link(last)
            v.tensor_scalar(VEG[:], MVG[:, :, 1], GN_EPS, None, ALU.add).then_inc(s_vg, 1)
            dve.wait_ge(s_rg, 1)
            v.scalar_tensor_tensor(NBG[:], MVG[:, :, 0], -1.0, RSG[:], ALU.mult, ALU.mult).then_inc(s_nb, 1)
            dve.wait_ge(ld["gb"], 32)
            dve.wait_ge(s_const, 1)
            dve.wait_ge(s_wrc, 4)
            for i in range(B + 2):
                a, s = i, i - 2
                if a < B:
                    dve.wait_ge(s_yn, a + 1)
                    link(v.tensor_tensor(Y0[:], YN[:, a, :], GAM[:], ALU.mult))
                    link(v.tensor_tensor(Y1[:], Y0[:], BET[:], ALU.add))
                    ge(dve, s_zt, a - 1)
                    v.tensor_tensor(Z[:, a % 2, :], Y1[:], WR[:, a, :], ALU.mult).then_inc(s_z, 1)
                if 0 <= s < B:
                    lg = PS[:, LOGIT, 0:E]
                    dve.wait_ge(s_lg, s + 1)
                    ge(dve, s_ex, s)
                    v.tensor_reduce(NM[:], lg, AX.X, ALU.max, negate=True).then_inc(s_nm, 1)
                    dve.wait_ge(s_ex, s + 1)
                    link(v.reciprocal(RZ[:], ZS[:]))
                    link(v.tensor_scalar(SC[:], EX[:], RZ[:, 0:1], None, ALU.mult))
                    link(v.max(TOP[:], SC[:]))
                    v.tensor_reduce(TS[:], TOP[:, 0:TOPK], AX.X, ALU.add)
                    link(v.max_index(IDX[:], TOP[:], SC[:]))
                    v.tensor_copy(IDF[:, s % 2, :], IDX[:])
                    link(v.tensor_scalar(TS[:], TS[:], TOP_EPS, None, ALU.add))
                    link(v.reciprocal(RT[:], TS[:]))
                    v.tensor_scalar(PAY[:, s, :, 1].bitcast(f32), TOP[:, 0:TOPK], RT[:, 0:1], None, ALU.mult)
                    link(v.tensor_tensor(OH[:, s % 2, :, :], IOE[:].unsqueeze(1).to_broadcast([128, TOPK, E]),
                                         IDF[:, s % 2, 0:TOPK].unsqueeze(2).to_broadcast([128, TOPK, E]), ALU.is_equal))
                    ge(dve, s_rk, s - 1)
                    link(v.tensor_reduce(M[:, s % 2, :], OH[:, s % 2, :, :].rearrange("p j e -> p e j"), AX.X, ALU.add))
                    v.tensor_tensor(MS[:, s + 1, :], MS[:, s, :], M[:, s % 2, :], ALU.add).then_inc(s_m, 1)
                    dve.wait_ge(s_sex, s + 1)
                    link(v.tensor_scalar(SSG[:], SEX[:], 1.0, None, ALU.add))
                    link(v.reciprocal(SRC[:], SSG[:]))
                    link(v.tensor_tensor(SSG[:], PS[:, GATE, 0:SF], SRC[:], ALU.mult))
                    ge(dve, s_st, s)
                    v.tensor_tensor(SAC[:], SSG[:], PS[:, UP, 0:SF], ALU.mult).then_inc(s_sact, 1)
                if a < B:
                    dve.wait_ge(s_wo, a + 1)
                    v.tensor_tensor(X[:, a, :], PS[:, WO, 0:D], X[:, a, :], ALU.add).then_inc(s_x2, 1)
                    dve.wait_ge(s_x2, a + 1)
                    link(v.bn_stats(ST2[:], X[:, a, :]))
                    link(v.bn_aggr(MV2[:], ST2[:]))
                    v.tensor_scalar(VE2[:], MV2[:, 1:2], LN_EPS, None, ALU.add).then_inc(s_v2, 1)
                if 0 <= s < B:
                    dve.wait_ge(s_rk, s + 1)
                    rk = PS[:, RANK, 0:E]
                    link(v.tensor_tensor(SEL[:], OH[:, s % 2, :, :], rk.unsqueeze(1).to_broadcast([128, TOPK, E]), ALU.mult))
                    link(v.tensor_reduce(RK[:], SEL[:], AX.X, ALU.add))
                    v.scalar_tensor_tensor(SLOT[:, s, :], RK[:], float(E), IDF[:, s % 2, 0:TOPK],
                                           ALU.mult, ALU.add).then_inc(s_slot, 1)
                    dve.wait_ge(s_sd, s + 1)
                    v.tensor_tensor(X[:, s, :], PS[:, SDB, 0:D], X[:, s, :], ALU.add).then_inc(s_xs, 1)
                if a < B:
                    dve.wait_ge(s_r2, a + 1)
                    v.tensor_scalar(HN[:, a, :], X[:, a, :], MV2[:, 0:1], RS2[:, 0:1],
                                    ALU.subtract, ALU.mult).then_inc(s_h, 1)
            dve.wait_ge(s_cnt, 1)
            link(v.tensor_tensor(OVF[:].rearrange("p (k e) -> p k e", e=E),
                                 PS[:, 0, 0:E].unsqueeze(1).to_broadcast([128, MAXE - 1, E]),
                                 THR[:].rearrange("p (k e) -> p k e", e=E), ALU.is_gt))
            link(v.tensor_tensor_scan(PRE[:], OVF[:], ZERO[:, 0:COLS], 0.0, ALU.add, ALU.add))
            link(v.tensor_scalar(LE[:], PRE[:], PM64[:, 0:1], 0.0, ALU.is_le, ALU.add, accum_out=CNT[:, 0:1]))
            link(v.tensor_tensor(CNT[:], CNT[:], PMIN[:], ALU.add))
            link(v.tensor_copy(LST[:, 0:1], CNT[:]))
            v.tensor_scalar(TT[:], PRE[0:1, COLS - 1:COLS], float(E), None, ALU.add)
            v.tensor_scalar(LST[:, 1:2], LST[:, 0:1], E - 1, None, ALU.bitwise_and).then_inc(s_list, 1)

            def entries(t, w, col):
                v.tensor_copy(IDR[:, w % U, :], TBL[:, bass.ds(col * 2, 2)] if not isinstance(col, int)
                              else TBL[:, 2 * col:2 * col + 2]).then_inc(s_id, 1)

            def hidden(t, w):
                ge(dve, s_sg, t + (w + 1))
                ge(dve, s_at, t + (w - 1))
                v.scalar_tensor_tensor(AC[:, w % 2, :], SG[:, w % 2, :], IDR[:, w % U, 1:2].bitcast(f32),
                                       PS[:, 2 + w % 2, F:2 * F], ALU.mult, ALU.mult).then_inc(s_act, 1)

            def step(i, u, listed):
                t = i * U
                ge(dve, s_at, t + (u + 1))
                ge(dve, s_d, t + (u - 1))
                v.tensor_copy(ATT[:, u % 2, :, :],
                              PS[0:FC, 4 + u % 2, 0:256].rearrange("p (c n) -> p c n", c=2)).then_inc(s_atc, 1)
                hidden(t, u + 1)
                w = u + LOOK_ID
                ge(dve, s_acc[(w - U) % 2], i * (16 * U // 2) + 16 * ((w - U) // 2 + 1))
                if listed:
                    col = dve.value_load(LROW[0:1, bass.ds(i * (2 * U) + 2 * w, 1)], min_val=0, max_val=BLK * E - 1)
                else:
                    col = t + w
                entries(t, w, col)

            dve.wait_ge(s_tbl, 16)
            for w in range(LOOK_ID):
                entries(0, w, w)
            dve.wait_ge(s_id, LOOK_ID)
            hidden(0, 0)
            dve.wait_ge(s_list, 1)
            T = dve.value_load(TT[0:1, 0:1], min_val=E, max_val=TILES - 1)
            for u in range(U):
                step(0, u, False)
            with dve.Fori(1, E // U - 1) as i:
                for u in range(U):
                    step(i, u, False)
            dve.wait_ge(s_lrow, 16)
            with dve.Fori(E // U - 1, TILES // U) as i:
                for u in range(U):
                    with dve.If(i * U + u < T):
                        step(i, u, True)

        @block.tensor
        def _(pe):
            mm, tr = nc.tensor.matmul, nc.tensor.transpose
            pe.wait_ge(ld["wh"], 16)
            pe.wait_ge(ld["ctx"], 16)
            for j in range(4):
                mm(PS[:, j, :], WH[:, j % 2, :], CT[:, j % 2, (j // 2) * HALF:(j // 2 + 1) * HALF],
                   start=True, stop=True).then_inc(s_kt, 1)
            pe.wait_ge(ld["cst"], 16)
            for g in range(4):
                pe.wait_ge(s_ktc, 2 * (g // 2) + 2)
                for h in range(H):
                    for b in range(2):
                        last = tr(PS[:, 4 + g, (h * 2 + b) * 128:(h * 2 + b + 1) * 128],
                                  KT[:, h, (2 * g + b) * S:(2 * g + b + 1) * S], IDN)
                last.then_inc(s_v, 1)
            pe.wait_ge(s_ktc, 4)
            for g in range(4):
                pe.wait_ge(s_xn, 2 * g + 2)
                for k in range(KD):
                    for b in range(2):
                        last = tr(PS[:, g, (k * 2 + b) * 128:(k * 2 + b + 1) * 128],
                                  XN[:, 2 * g + b, k * 128:(k + 1) * 128], IDN)
                last.then_inc(s_xt, 1)
            for j in range(4):
                pe.wait_ge(s_vc, j + 1)
                pe.wait_ge(s_xtc, 2 * (j // 2) + 2)
                mm(PS[:, 4 + j, :], WH[:, j % 2, :], XNT[:, j % 2, (j // 2) * HALF:(j // 2 + 1) * HALF],
                   start=True, stop=True).then_inc(s_q, 1)

            def gate(g):
                for b in (2 * g, 2 * g + 1):
                    for k in range(KD):
                        last = mm(PS[:, 1 + g % 3, (b % 2) * D:(b % 2 + 1) * D], XNT[:, k, b * S:(b + 1) * S],
                                  WGT[:, k, :], start=(k == 0), stop=(k == KD - 1))
                last.then_inc(s_wr, 1)

            pe.wait_ge(ld["wg"], 16)
            gate(0)
            pe.wait_ge(s_qc, 4)
            for h in range(H):
                for b in range(B):
                    last = mm(PS[:, 0, h * S:(h + 1) * S], KT[:, h, b * S:(b + 1) * S], QT[:, h, b * S:(b + 1) * S],
                              start=(b == 0), stop=(b == B - 1))
            last.then_inc(s_sc, 1)
            gate(1)
            gate(2)

            def attend(half):
                for h in range(H):
                    last = mm(PS[:, 4 + 2 * half + h, :], AT[:, h, :], V[:, h, 4 * half:4 * half + 4, :].rearrange("p b e -> p (b e)"),
                              start=True, stop=True)
                last.then_inc(s_o, 1)

            pe.wait_ge(s_a, 1)
            attend(0)
            attend(1)
            pe.wait_ge(s_wrc, 1)
            gate(3)
            pe.wait_ge(s_wrc, 4)
            for n in ("wo", "gw", "wsg", "wsd"):
                pe.wait_ge(ld[n], 16)
            pe.wait_ge(s_const, 1)
            for i in range(B + 2):
                a, r, s = i, i - 1, i - 2
                if a < B:
                    pe.wait_ge(s_z, a + 1)
                    ge(pe, s_ztc, a)
                    for k in range(KD):
                        last = tr(PS[:, ZTB, k * 128:(k + 1) * 128], Z[:, a % 2, k * 128:(k + 1) * 128], IDN)
                    last.then_inc(s_zt, 1)
                if 0 <= s < B:
                    pe.wait_ge(s_htc, s + 1)
                    ge(pe, s_stc, s)
                    if s == 0:
                        pe.wait_ge(s_yn, B)
                    ge(pe, s_sact, s)
                    for g in range(2):
                        for k in range(KD):
                            last = mm(PS[:, GATE + g, 0:SF], HT[:, k, s * S:(s + 1) * S], WSG[:, k, g * SF:(g + 1) * SF],
                                      start=(k == 0), stop=(k == KD - 1))
                    last.then_inc(s_sgu, 1)
                    pe.wait_ge(s_m, s + 1)
                    ge(pe, s_slot, s)
                    rk = PS[:, RANK, 0:E]
                    mm(rk, TRI, M[:, s % 2, :], start=True, stop=False)
                    mm(rk, ONE[:], MS[:, s, :], start=False, stop=True).then_inc(s_rk, 1)
                if a < B:
                    pe.wait_ge(s_ztc, a + 1)
                    ge(pe, s_x2, a)
                    for k in range(KD):
                        last = mm(PS[:, WO, 0:D], ZT[:, a % 2, k, :], WOT[:, k, :],
                                  start=(k == 0), stop=(k == KD - 1))
                    last.then_inc(s_wo, 1)
                if 0 <= s < B:
                    pe.wait_ge(s_sact, s + 1)
                    for c in range(SF // FC):
                        last = tr(PS[0:FC, GATE, c * 128:(c + 1) * 128], SAC[:, c * FC:(c + 1) * FC], IDN)
                    last.then_inc(s_st, 1)
                if 0 <= r < B:
                    pe.wait_ge(s_h, r + 1)
                    ge(pe, s_htc, r)
                    for k in range(KD):
                        last = tr(PS[:, HTB, k * 128:(k + 1) * 128], HN[:, r, k * 128:(k + 1) * 128], IDN)
                    last.then_inc(s_ht, 1)
                if 0 <= s < B:
                    pe.wait_ge(s_stc, s + 1)
                    ge(pe, s_xs, s)
                    for c in range(SF // FC):
                        last = mm(PS[:, SDB, 0:D], SACT[:, c, :], WSD[:, c, :],
                                  start=(c == 0), stop=(c == SF // FC - 1))
                    last.then_inc(s_sd, 1)
                if 0 <= r < B:
                    pe.wait_ge(s_htc, r + 1)
                    ge(pe, s_ex, r)
                    for k in range(KD):
                        last = mm(PS[:, LOGIT, 0:E], HT[:, k, r * S:(r + 1) * S], GWT[:, k, :],
                                  start=(k == 0), stop=(k == KD - 1))
                    last.then_inc(s_lg, 1)
            pe.wait_ge(s_slot, B)
            mm(PS[:, 0, 0:E], ONE[:], MS[:, B, :], start=True, stop=True).then_inc(s_cnt, 1)

            def rows(t, w):
                g = w % LOOK_G
                for k in range(KD):
                    last = tr(PS[:, w % 2, k * 128:(k + 1) * 128], XG[:, g, k * 128:(k + 1) * 128], IDN)
                last.then_inc(s_xg, 1)

            def gate_up(t, w, slot):
                for k in range(KD):
                    rhs = (WGU[:, slot * 2 * SF + k * SF:slot * 2 * SF + (k + 1) * SF] if isinstance(slot, int)
                           else WGU[:, bass.ds(slot * (2 * SF) + k * SF, SF)])
                    last = mm(PS[:, 2 + w % 2, 0:SF], XT[:, w % 2, k, :], rhs, start=(k == 0), stop=(k == KD - 1))
                last.then_inc(s_gu, 1)

            def step(i, u):
                t = i * U
                pe.wait_ge(s_act, t + (u + 1))
                ge(pe, s_atc, t + (u - 1))
                for c in range(2):
                    last = tr(PS[0:FC, 4 + u % 2, c * 128:(c + 1) * 128], AC[:, u % 2, c * FC:(c + 1) * FC], IDN)
                last.then_inc(s_at, 1)
                w = u + 2
                pe.wait_ge(s_g[w % LOOK_G], i * (16 * U // LOOK_G) + 16 * (w // LOOK_G + 1))
                pe.wait_ge(s_xgc, t + (u + 1))
                rows(t, w)
                w = u + 1
                pe.wait_ge(s_xgc, t + (w + 1))
                pe.wait_ge(s_w[w % U], i * 32 + 32 * (w // U + 1))
                pe.wait_ge(s_act, t + w)
                gate_up(t, w, (i * U + w) % R)
                pe.wait_ge(s_atc, t + (u + 1))
                ge(pe, s_y, t + (u - 1))
                slot = (i * U + u) % R
                for c in range(2):
                    rhs = (WDN[:, slot * 2 * D + c * D:slot * 2 * D + (c + 1) * D] if isinstance(slot, int)
                           else WDN[:, bass.ds(slot * (2 * D) + c * D, D)])
                    last = mm(PS[:, 6 + u % 2, 0:D], ATT[:, u % 2, c, :], rhs, start=(c == 0), stop=(c == 1))
                last.then_inc(s_d, 1)

            pe.wait_ge(s_list, 1)
            for w in range(2):
                pe.wait_ge(s_g[w], 16)
                rows(0, w)
            pe.wait_ge(s_xgc, 1)
            pe.wait_ge(s_w[0], 32)
            gate_up(0, 0, 0)
            T = pe.value_load(TT[0:1, 0:1], min_val=E, max_val=TILES - 1)
            for u in range(U):
                step(0, u)
            with pe.Fori(1, E // U - 1) as i:
                for u in range(U):
                    step(i, u)
            with pe.Fori(E // U - 1, TILES // U) as i:
                for u in range(U):
                    with pe.If(i * U + u < T):
                        step(i, u)


def shape_constants():
    f = np.float32
    gam = (1.0 - 2.0 ** (-5.0 - np.arange(H, dtype=f))).astype(f)
    idx = np.arange(S, dtype=f)
    expo = idx[None, :] - idx[:, None]
    d = np.where(expo[None] <= 0, gam[:, None, None] ** expo[None], f(0)).astype(f)
    d = (d / np.sqrt(d.sum(axis=-1, dtype=f))[:, None, :]).astype(f)
    mask_t = d.transpose(2, 0, 1).reshape(S, H * S)
    tri = np.triu(np.ones((128, 128), f), 1)
    return np.ascontiguousarray(np.concatenate([np.eye(128, dtype=f), tri, mask_t], axis=1), dtype=f)


def kernel(**inputs):
    import concourse.bacc as bacc
    from concourse.bass_utils import run_bass_kernel_spmd

    a = {k: np.asarray(v) for k, v in inputs.items()}
    chunk = lambda w, p: w.reshape(-1, p, w.shape[-1]).transpose(1, 0, 2)
    arrays = {
        "x": a["x"].transpose(1, 0, 2),
        "ctxT": a["ctx_2048"].reshape(N, H, HD).transpose(2, 1, 0),
        "Wh": a["L0_xattn_Wh"].transpose(1, 0, 2),
        "wg": chunk(a["L0_xattn_wg_w"], 128),
        "wo": chunk(a["L0_xattn_wo_w"], 128),
        "gam": np.broadcast_to(a["L0_xattn_gn_gamma"], (128, D)),
        "bet": np.broadcast_to(a["L0_xattn_gn_beta"], (128, D)),
        "gw": chunk(a["L0_ffn_gate_w"].T, 128),
        "wgu": a["L0_ffn_w_gate_up"].reshape(E, SF, KD, 128).transpose(0, 3, 2, 1).reshape(E, 128, KD * SF),
        "wdn": a["L0_ffn_w_down"].reshape(E, D, 2, FC).transpose(0, 3, 2, 1).reshape(E, FC, 2 * D),
        "wsg": chunk(a["L0_ffn_ws_gate_up"].T, 128),
        "wsd": chunk(a["L0_ffn_ws_down"].T, FC),
        "cst": shape_constants(),
    }
    arrays = {k: np.ascontiguousarray(v) for k, v in arrays.items()}
    nc = bacc.Bacc("TRN2", target_bir_lowering=False, num_devices=1)
    f32 = mybir.dt.float32
    args = [nc.dram_tensor("in_" + k, v.shape, f32, kind="ExternalInput").ap() for k, v in arrays.items()]
    out = nc.dram_tensor("out_rows", (N + 128, D), f32, kind="ExternalOutput").ap()
    program(nc, *args, out)
    r = run_bass_kernel_spmd(nc, [{"in_" + k: v for k, v in arrays.items()}], core_ids=[0])
    return np.asarray(r.results[0]["out_rows"])[:N].reshape(B, S, D)
```

```python
import numpy as np
import concourse.bass as bass
from concourse import mybir
from contextlib import ExitStack

B, S, D = 8, 128, 256
N = B * S
H, HD = 2, 128
KD = D // 128
E, F, TOPK = 64, 176, 6
SF = 2 * F
FC = 88
LN_EPS, GN_EPS, TOP_EPS = 1e-5, 1e-3, 1e-20
MAXE = N // 128
BLK = MAXE + 1
COLS = (MAXE - 1) * E
EXTRA = (N * TOPK) // 128
TILES = E + EXTRA
R = 16
U = 8
LOOK_ID, LOOK_G, LOOK_R = 5, 4, 3
STEPS = B + 7
K_BANK, V_BANK, W_BANK, SCORE = (2, 3, 0, 1), (4, 5, 0, 1), (2, 0, 1, 2), 3
HALF = 4 * S


def program(nc, x, ctxT, Wh, wg, wo, gam, bet, gw, wgu, wdn, wsg, wsd, cst, out):
    f32, i32, u32 = mybir.dt.float32, mybir.dt.int32, mybir.dt.uint32
    ALU, ACT, AX = mybir.AluOpType, mybir.ActivationFunctionType, mybir.AxisListType

    tbl = nc.dram_tensor("slot_table", [BLK * 128, E, 2], i32).ap()
    hbuf = nc.dram_tensor("h_rows", [N + 128, D], f32).ap()
    acc1 = nc.dram_tensor("acc_odd", [N + 128, D], f32).ap()
    lst_d = nc.dram_tensor("tile_list", [128, 2], i32).ap()

    with ExitStack() as ctx:
        def sb(name, shape, dt=f32):
            return ctx.enter_context(nc.sbuf_tensor(name, shape, dt))

        def sem(name):
            return ctx.enter_context(nc.semaphore(name))

        X = sb("X", [128, B, D])
        CT = sb("CT", [128, H, N])
        XN = sb("XN", [128, B, D])
        XNT = sb("XNT", [128, KD, N])
        QT = sb("QT", [128, H, N])
        KT = sb("KT", [128, H, N])
        V = sb("V", [128, H, B, HD])
        HT, WR = CT, XN
        SH = XNT[:, :, :].rearrange("p k n -> p (k n)").rearrange("p (b d) -> p b d", b=B)
        YN = KT[:, :, :].rearrange("p h n -> p (h n)").rearrange("p (b d) -> p b d", b=B)
        HN = QT[:, :, :].rearrange("p h n -> p (h n)").rearrange("p (b d) -> p b d", b=B)
        WH = sb("WH", [128, H, HD])
        WGT = sb("WGT", [128, KD, D])
        WOT = sb("WOT", [128, KD, D])
        GWT = sb("GWT", [128, KD, E])
        WSG = sb("WSG", [128, KD, 2 * SF])
        WSD = sb("WSD", [FC, SF // FC, D])
        GAM = sb("GAM", [128, D])
        BET = sb("BET", [128, D])
        CST = sb("CST", [128, 512])
        IDN, TRI, MASK = CST[:, 0:128], CST[:, 128:256], CST[:, 256:512]
        ONE = sb("ONE", [128, 128])
        IOE = sb("IOE", [128, E])
        THR = sb("THR", [128, COLS])
        PM64 = sb("PM64", [128, 1])
        PMIN = sb("PMIN", [128, 1])
        ZERO = sb("ZERO", [128, 512])
        INIT = sb("INIT", [128, E, 2], i32)
        PAY = sb("PAY", [128, B, TOPK, 2], i32)
        SLOT = sb("SLOT", [128, B, TOPK], i32)
        AT = sb("AT", [128, H, S])
        AT0 = sb("AT0", [128, H, S])
        AT1 = sb("AT1", [128, H, S])
        NHALF = sb("NHALF", [128, 1])
        ST1 = sb("ST1", [128, B, 6])
        MV1 = sb("MV1", [128, B, 2])
        RS1 = sb("RS1", [128, B])
        STG = sb("STG", [128, B, 6])
        MVG = sb("MVG", [128, B, 2])
        VE1 = sb("VE1", [128, B])
        VEG = sb("VEG", [128, B])
        VE2 = sb("VE2", [128, 1])
        RSG = sb("RSG", [128, B])
        NBG = sb("NBG", [128, B])
        ST2 = sb("ST2", [128, 6])
        MV2 = sb("MV2", [128, 2])
        RS2 = sb("RS2", [128, 1])
        Y0 = sb("Y0", [128, D])
        Y1 = sb("Y1", [128, D])
        Z = sb("Z", [128, 2, D])
        ZT = sb("ZT", [128, 2, KD, 128])
        NM = sb("NM", [128, 1])
        EX = sb("EX", [128, E])
        ZS = sb("ZS", [128, 1])
        TOP = sb("TOP", [128, 8])
        IDX = sb("IDX", [128, 8], u32)
        IDF = sb("IDF", [128, 2, 8])
        TS = sb("TS", [128, 1])
        TD = sb("TD", [128, 1])
        RT = sb("RT", [128, 1])
        OH = sb("OH", [128, 2, TOPK, E])
        SEL = sb("SEL", [128, TOPK, E])
        RK = sb("RK", [128, TOPK])
        M = sb("M", [128, 2, E])
        MS = sb("MS", [128, B + 1, E])
        SEX = sb("SEX", [128, SF])
        SSG = sb("SSG", [128, SF])
        SAC = sb("SAC", [128, SF])
        SACT = sb("SACT", [FC, SF // FC, 128])
        OVF = sb("OVF", [128, COLS])
        PRE = sb("PRE", [128, COLS])
        LE = sb("LE", [128, COLS])
        CNT = sb("CNT", [128, 1])
        LST = sb("LST", [128, 2], i32)
        TT = sb("TT", [1, 1], i32)
        LROW = sb("LROW", [1, 256], i32)
        TBL = sb("TBL", [128, BLK * E * 2], i32)
        IDR = sb("IDR", [128, U, 2], i32)
        XG = sb("XG", [128, LOOK_G, D])
        XT = sb("XT", [128, 2, KD, 128])
        SG = sb("SG", [128, 2, F])
        AC = sb("AC", [128, 2, F])
        ATT = sb("ATT", [FC, 2, 2, 128])
        YS = sb("YS", [128, 4, D])
        WGU = sb("WGU", [128, R * 2 * SF])
        WDN = sb("WDN", [FC, R * 2 * D])
        RANK, ZH, WO, STB, LOGIT, GATE, UP, SDB = range(8)
        PS = ctx.enter_context(nc.psum_tensor("PS", [128, 8, 512], f32))

        ld = {n: sem("ld_" + n) for n in ("ctx", "wh", "x0", "x1", "cst", "wg", "wo", "gb", "gw", "wsg", "wsd")}
        s_const, s_init = sem("s_const"), sem("s_init")
        s_kt, s_ktc, s_v, s_vc, s_xn, s_xt, s_xtc, s_q, s_qc = (
            sem(n) for n in ("s_kt", "s_ktc", "s_v", "s_vc", "s_xn", "s_xt", "s_xtc", "s_q", "s_qc"))
        s_sc, s_a, s_wr, s_wrc, s_o = (sem(n) for n in ("s_sc", "s_a", "s_wr", "s_wrc", "s_o"))
        s_z, s_zt, s_ztc, s_wo, s_x2, s_h, s_ht, s_htc = (
            sem(n) for n in ("s_z", "s_zt", "s_ztc", "s_wo", "s_x2", "s_h", "s_ht", "s_htc"))
        s_lg, s_nm, s_ex, s_m, s_rk, s_slot = (sem(n) for n in ("s_lg", "s_nm", "s_ex", "s_m", "s_rk", "s_slot"))
        s_sgu, s_sex, s_sact, s_st, s_stc, s_sd, s_shc = (
            sem(n) for n in ("s_sgu", "s_sex", "s_sact", "s_st", "s_stc", "s_sd", "s_shc"))
        s_v1, s_r1, s_vg, s_rg, s_nb, s_yn, s_v2, s_r2 = (
            sem(n) for n in ("s_v1", "s_r1", "s_vg", "s_rg", "s_nb", "s_yn", "s_v2", "s_r2"))
        s_cnt, s_list, s_lstd, s_lrow = sem("s_cnt"), sem("s_list"), sem("s_lstd"), sem("s_lrow")
        s_tsc, s_tbl, s_hst, s_ost = sem("s_tsc"), sem("s_tbl"), sem("s_hst"), sem("s_ost")
        s_dve = sem("s_dve")
        s_w = [sem(f"s_w{u}") for u in range(U)]
        s_g = [sem(f"s_g{u}") for u in range(LOOK_G)]
        s_acc = [sem(f"s_acc{u}") for u in range(2)]
        s_id, s_xg, s_xgc, s_gu, s_sg, s_act, s_at, s_atc, s_d, s_y = (
            sem(n) for n in ("m_id", "m_xt", "m_xtc", "m_gu", "m_sg", "m_act", "m_at", "m_atc", "m_d", "m_y"))
        s_fin, s_turn, s_sp = sem("s_fin"), sem("s_turn"), sem("s_sp")

        block = ctx.enter_context(nc.Block())

        def ge(eng, s, v):
            if not isinstance(v, int) or v > 0:
                eng.wait_ge(s, v)

        def heads_of(b):
            return PS[:, 4 + 2 * (b // 4):6 + 2 * (b // 4), (b % 4) * HD:(b % 4 + 1) * HD]

        @block.sync
        def _(sp):
            for half in range(2):
                sp.dma_start(X[:, 4 * half:4 * half + 4, :], x[:, 4 * half:4 * half + 4, :]).then_inc(ld[f"x{half}"], 16)
            sp.dma_start(CST[:], cst).then_inc(ld["cst"], 16)
            sp.dma_start(WH[:], Wh).then_inc(ld["wh"], 16)
            sp.dma_start(CT[:], ctxT).then_inc(ld["ctx"], 16)
            sp.dma_start(WGT[:], wg).then_inc(ld["wg"], 16)
            sp.dma_start(WOT[:], wo).then_inc(ld["wo"], 16)
            sp.dma_start(GAM[:], gam).then_inc(ld["gb"], 16)
            sp.dma_start(BET[:], bet).then_inc(ld["gb"], 16)
            sp.dma_start(GWT[:], gw).then_inc(ld["gw"], 16)
            sp.dma_start(WSG[:], wsg).then_inc(ld["wsg"], 16)
            sp.dma_start(WSD[:], wsd).then_inc(ld["wsd"], 16)
            sp.wait_ge(s_const, 1)
            blocks = "(k p) e c -> p k (e c)"
            sp.dma_start(tbl.rearrange(blocks, p=128),
                         INIT[:].rearrange("p e c -> p (e c)").unsqueeze(1).to_broadcast([128, BLK, 2 * E])).then_inc(s_init, 16)
            sp.dma_start(acc1[N:N + 128, :], ZERO[:, 0:D]).then_inc(s_init, 16)
            sp.dma_start(hbuf[N:N + 128, :], ZERO[:, 0:D]).then_inc(s_init, 16)
            sp.dma_start(out[N:N + 128, :], ZERO[:, 0:D]).then_inc(s_init, 16)

            def load(slot, u, e):
                sp.dma_start(WGU[:, slot * 2 * SF:(slot + 1) * 2 * SF], wgu[e]).then_inc(s_w[u], 16)
                sp.dma_start(WDN[:, slot * 2 * D:(slot + 1) * 2 * D], wdn[e]).then_inc(s_w[u], 16)

            def load_dyn(i, u, e):
                slot = (i % 2) * U + u
                sp.dma_start(WGU[:, bass.ds(slot * (2 * SF), 2 * SF)],
                             wgu[bass.ds(e, 1)].rearrange("o p n -> (o p) n")).then_inc(s_w[u], 16)
                sp.dma_start(WDN[:, bass.ds(slot * (2 * D), 2 * D)],
                             wdn[bass.ds(e, 1)].rearrange("o p n -> (o p) n")).then_inc(s_w[u], 16)

            for t in range(R):
                ge(sp, s_w[t % U], 32 * (t // U))
                load(t, t % U, t)
            for b in range(B):
                sp.wait_ge(s_x2, b + 1)
                sp.dma_start(out[b * S:(b + 1) * S, :], X[:, b, :]).then_inc(s_ost, 16)
                sp.wait_ge(s_h, b + 1)
                sp.dma_start(hbuf[b * S:(b + 1) * S, :], HN[:, b, :]).then_inc(s_hst, 16)
            for b in range(B):
                sp.wait_ge(s_shc, b + 1)
                sp.dma_start(acc1[b * S:(b + 1) * S, :], SH[:, b, :]).then_inc(s_ost, 16)
            sp.wait_ge(s_list, 1)
            sp.dma_start(lst_d, LST[:]).then_inc(s_lstd, 16)
            sp.wait_ge(s_lstd, 16)
            sp.dma_start(LROW[:], lst_d.rearrange("(o t) c -> o (t c)", o=1)).then_inc(s_lrow, 16)
            T = sp.value_load(TT[0:1, 0:1], min_val=E, max_val=TILES - 1)
            sp.wait_ge(s_lrow, 16)
            with sp.Fori(R // U, E // U) as i:
                for u in range(U):
                    sp.wait_ge(s_d, i * U + (u - R + 1))
                    sp.sem_inc(s_sp)
                    sp.wait_ge(s_w[u], i * 32)
                    sp.sem_inc(s_sp)
                    load_dyn(i, u, i * U + u)
            with sp.Fori(E // U, TILES // U) as i:
                for u in range(U):
                    with sp.If(i * U + (u - 1) < T):
                        e = sp.value_load(LROW[0:1, bass.ds(i * (2 * U) + (2 * u + 1), 1)], min_val=0, max_val=E - 1)
                        sp.wait_ge(s_d, i * U + (u - R + 1))
                        sp.sem_inc(s_sp)
                        sp.wait_ge(s_w[u], i * 32)
                        sp.sem_inc(s_sp)
                        load_dyn(i, u, e)

        @block.gpsimd
        def _(pool):
            nc.gpsimd.memset(INIT[:], 0).then_inc(s_init, 1)
            pool.wait_ge(s_init, 1)
            nc.gpsimd.iota(INIT[:, :, 0], [[0, E]], base=N, channel_multiplier=1)
            nc.gpsimd.memset(ZERO[:], 0.0)
            nc.gpsimd.memset(ONE[:], 1.0)
            nc.gpsimd.memset(MS[:, 0, :], 0.0)
            nc.gpsimd.memset(NHALF[:], -0.5)
            nc.gpsimd.iota(PAY[:, :, :, 0], [[S, B], [0, TOPK]], base=0, channel_multiplier=1)
            nc.gpsimd.iota(IOE[:], [[1, E]], base=0, channel_multiplier=0, allow_small_or_imprecise_dtypes=True)
            nc.gpsimd.iota(THR[:], [[128, MAXE - 1], [0, E]], base=128, channel_multiplier=0,
                           allow_small_or_imprecise_dtypes=True)
            nc.gpsimd.iota(PM64[:], [[0, 1]], base=-E, channel_multiplier=1,
                           allow_small_or_imprecise_dtypes=True).then_inc(s_init, 1)
            pool.wait_ge(s_init, 2)
            nc.gpsimd.tensor_scalar(PMIN[:], PM64[:], float(E), float(E), ALU.add, ALU.min).then_inc(s_const, 1)
            minus_half = NHALF[:, 0:1].to_broadcast([128, 4])
            for half in range(2):
                c = slice(4 * half, 4 * half + 4)
                pool.wait_ge(s_v1, half + 1)
                nc.gpsimd.tensor_tensor(RS1[:, c], VE1[:, c], minus_half, ALU.pow).then_inc(s_r1, 1)
            for half in range(2):
                c = slice(4 * half, 4 * half + 4)
                pool.wait_ge(s_vg, half + 1)
                nc.gpsimd.tensor_tensor(RSG[:, c], VEG[:, c], minus_half, ALU.pow).then_inc(s_rg, 1)
            for i in range(B + 4):
                b, k = i - 1, i - 4
                for j in range(TOPK):
                    if j == 2 and 0 <= b < B:
                        pool.wait_ge(s_v2, b + 1)
                        ge(pool, s_h, b)
                        nc.gpsimd.tensor_tensor(RS2[:], VE2[:], NHALF[:], ALU.pow).then_inc(s_r2, 1)
                    if k == 0 and j == 0:
                        pool.wait_ge(s_init, 2 + 4 * 16)
                    if 0 <= k:
                        if j == 0:
                            pool.wait_ge(s_slot, k + 1)
                        pool.indirect_dma_start(tbl.rearrange("r e c -> (r e) c"),
                                                bass.IndirectOffsetOnAxis(ap=SLOT[:, k, j:j + 1], axis=0),
                                                PAY[:, k, j, :], None).then_inc(s_tsc, 16)

            def gather(g, idr):
                pool.indirect_dma_start(XG[:, g, :], None, hbuf,
                                        bass.IndirectOffsetOnAxis(ap=IDR[:, idr, 0:1], axis=0)).then_inc(s_g[g], 16)

            def step(i, u):
                t = i * U
                ge(pool, s_id, t + (u + LOOK_G + 1))
                ge(pool, s_xg, t + (u + 1))
                pool.sem_inc(s_turn)
                gather((u + LOOK_G) % LOOK_G, (u + LOOK_G) % U)
                ge(pool, s_y, t + (u + 1))
                ge(pool, s_acc[u % 2], i * (16 * U // 2) + 16 * (u // 2))
                pool.sem_inc(s_turn)
                pool.indirect_dma_start((out, acc1)[u % 2],
                                        bass.IndirectOffsetOnAxis(ap=IDR[:, u, 0:1], axis=0),
                                        YS[:, u % 4, :], None, compute_op=ALU.add).then_inc(s_acc[u % 2], 16)

            pool.wait_ge(s_hst, 16 * B)
            for t in range(LOOK_G):
                ge(pool, s_id, t + 1)
                gather(t, t)
            pool.wait_ge(s_ost, 32 * B)
            T = pool.value_load(TT[0:1, 0:1], min_val=E, max_val=TILES - 1)
            for u in range(U):
                step(0, u)
            with pool.Fori(1, E // U - 1) as i:
                for u in range(U):
                    step(i, u)
            with pool.Fori(E // U - 1, TILES // U) as i:
                for u in range(U):
                    with pool.If(i * U + u < T):
                        step(i, u)
            for g in range(LOOK_G):
                pool.wait_ge(s_g[g], (T + (2 * LOOK_G - 1 - g)) // LOOK_G * 16)
            pool.wait_ge(s_acc[0], (T + 1) // 2 * 16)
            pool.wait_ge(s_acc[1], T // 2 * 16)
            pool.sem_inc(s_turn)
            pool.dma_start(out[0:N, :], acc1[0:N, :], accum_op=ALU.add, max_dma_last_dim=8192).then_inc(s_fin, 16)
            pool.wait_ge(s_fin, 16)

        @block.scalar
        def _(act):
            def qk(dst, bank, j, s, c):
                act.wait_ge(s, j + 1)
                nc.scalar.copy(dst[:, j % 2, (j // 2) * HALF:(j // 2 + 1) * HALF], PS[:, bank, :]).then_inc(c, 1)

            def relu_gate(g):
                act.wait_ge(s_wr, g + 1)
                nc.scalar.activation(WR[:, 2 * g:2 * g + 2, :],
                                     PS[:, W_BANK[g], :].rearrange("p (b d) -> p b d", b=2), ACT.Relu).then_inc(s_wrc, 1)

            def normalise(half):
                act.wait_ge(s_nb, half + 1)
                for b in range(4 * half, 4 * half + 4):
                    nc.scalar.activation(YN[:, b, :].rearrange("p (h e) -> p h e", h=H), heads_of(b), ACT.Identity,
                                         bias=NBG[:, b:b + 1], scale=RSG[:, b:b + 1]).then_inc(s_yn, 1)

            for j in range(2):
                qk(QT, 4 + j, j, s_q, s_qc)
            for j in range(4):
                qk(KT, K_BANK[j], j, s_kt, s_ktc)
            for j in range(2, 4):
                qk(QT, 4 + j, j, s_q, s_qc)
            for g in range(4):
                act.wait_ge(s_v, g + 1)
                nc.scalar.copy(V[:, :, 2 * g:2 * g + 2, :],
                               PS[:, V_BANK[g], :].rearrange("p (h b e) -> p h b e", h=H, b=2)).then_inc(s_vc, 1)
            relu_gate(0)
            normalise(0)
            relu_gate(1)
            normalise(1)
            relu_gate(2)
            relu_gate(3)
            for i in range(STEPS):
                if 0 <= i - 3 < B:
                    r = i - 3
                    act.wait_ge(s_nm, r + 1)
                    ge(act, s_m, r)
                    nc.scalar.activation(EX[:], PS[:, LOGIT, 0:E], ACT.Exp, bias=NM[:, 0:1],
                                         accum_out=ZS[:, 0:1]).then_inc(s_ex, 1)
                if 0 <= i - 5 < B:
                    s = i - 5
                    act.wait_ge(s_sgu, s + 1)
                    ge(act, s_sact, s)
                    nc.scalar.activation(SEX[:], PS[:, GATE, 0:SF], ACT.Tanh, scale=0.5).then_inc(s_sex, 1)
                if i < B:
                    act.wait_ge(s_zt, i + 1)
                    ge(act, s_wo, i - 1)
                    nc.scalar.copy(ZT[:, i % 2, :, :],
                                   PS[:, ZH, 0:256].rearrange("p (k n) -> p k n", k=KD)).then_inc(s_ztc, 1)
                if 0 <= i - 6 < B:
                    s = i - 6
                    act.wait_ge(s_st, s + 1)
                    ge(act, s_sd, s)
                    nc.scalar.copy(SACT[:], PS[0:FC, STB, :].rearrange("p (c n) -> p c n", c=SF // FC)).then_inc(s_stc, 1)
                if 0 <= i - 2 < B:
                    r = i - 2
                    act.wait_ge(s_ht, r + 1)
                    nc.scalar.copy(HT[:, :, r * S:(r + 1) * S],
                                   PS[:, ZH, 256:512].rearrange("p (k n) -> p k n", k=KD)).then_inc(s_htc, 1)
                if 0 <= i - 7 < B:
                    s = i - 7
                    act.wait_ge(s_sd, s + 1)
                    nc.scalar.copy(SH[:, s, :], PS[:, SDB, 0:D]).then_inc(s_shc, 1)
            act.wait_ge(s_tsc, 16 * TOPK * B)
            act.dma_start(TBL[:].rearrange("p (k n) -> p k n", k=BLK),
                          tbl.rearrange("(k p) e c -> p k (e c)", p=128)).then_inc(s_tbl, 16)

            def rows_in(t, v):
                ge(act, s_xg, t + (v + 1))
                ge(act, s_gu, t + (v - 1))
                nc.scalar.copy(XT[:, v % 2, :, :],
                               PS[:, v % 2, 0:256].rearrange("p (k n) -> p k n", k=KD)).then_inc(s_xgc, 1)

            def silu(t, v):
                ge(act, s_gu, t + (v + 1))
                ge(act, s_act, t + (v - 1))
                nc.scalar.activation(SG[:, v % 2, :], PS[:, 2 + v % 2, 0:F], ACT.Silu).then_inc(s_sg, 1)

            def step(i, u):
                t = i * U
                silu(t, u + 1)
                ge(act, s_d, t + (u + 1))
                ge(act, s_acc[u % 2], i * (16 * U // 2) + 16 * (u // 2 - 1))
                nc.scalar.copy(YS[:, u % 4, :], PS[:, 6 + u % 2, 0:D]).then_inc(s_y, 1)
                rows_in(t, u + LOOK_R)

            rows_in(0, 0)
            rows_in(0, 1)
            silu(0, 0)
            rows_in(0, 2)
            act.wait_ge(s_list, 1)
            T = act.value_load(TT[0:1, 0:1], min_val=E, max_val=TILES - 1)
            for u in range(U):
                step(0, u)
            with act.Fori(1, E // U - 1) as i:
                for u in range(U):
                    step(i, u)
            with act.Fori(E // U - 1, TILES // U) as i:
                for u in range(U):
                    with act.If(i * U + u < T):
                        step(i, u)

        @block.vector
        def _(dve):
            count = [0]

            def tick(ins):
                count[0] += 1
                ins.then_inc(s_dve, 1)
                return count[0]

            def need(n):
                dve.wait_ge(s_dve, n)

            def link(ins):
                need(tick(ins))

            v = nc.vector
            for half in range(2):
                c = slice(4 * half, 4 * half + 4)
                dve.wait_ge(ld[f"x{half}"], 16)
                for b in range(4 * half, 4 * half + 4):
                    n = tick(v.bn_stats(ST1[:, b, :], X[:, b, :]))
                need(n)
                for b in range(4 * half, 4 * half + 4):
                    n = tick(v.bn_aggr(MV1[:, b, :], ST1[:, b, :]))
                need(n)
                v.tensor_scalar(VE1[:, c], MV1[:, c, 1], LN_EPS, None, ALU.add).then_inc(s_v1, 1)
            for half in range(2):
                dve.wait_ge(s_r1, half + 1)
                for b in range(4 * half, 4 * half + 4):
                    v.tensor_scalar(XN[:, b, :], X[:, b, :], MV1[:, b, 0:1], RS1[:, b:b + 1],
                                    ALU.subtract, ALU.mult).then_inc(s_xn, 1)
                for g in range(2 * half, 2 * half + 2):
                    dve.wait_ge(s_xt, g + 1)
                    v.tensor_copy(XNT[:, :, g * 256:(g + 1) * 256],
                                  PS[:, g, :].rearrange("p (k n) -> p k n", k=KD)).then_inc(s_xtc, 1)
            dve.wait_ge(s_sc, 1)
            link(v.scalar_tensor_tensor(AT0[:].rearrange("p h s -> p (h s)"), PS[:, SCORE, 0:256],
                                        float(np.float32(1.0) / np.sqrt(np.float32(HD))), MASK, ALU.mult, ALU.mult))
            link(v.scalar_tensor_tensor(AT1[:], AT0[:], -1.0, AT0[:], ALU.mult, ALU.max))
            v.tensor_scalar(AT[:], AT1[:], 1.0, None, ALU.max).then_inc(s_a, 1)
            for half in range(2):
                c = slice(4 * half, 4 * half + 4)
                dve.wait_ge(s_o, half + 1)
                for b in range(4 * half, 4 * half + 4):
                    n = tick(v.bn_stats(STG[:, b, :], heads_of(b)))
                need(n)
                for b in range(4 * half, 4 * half + 4):
                    n = tick(v.bn_aggr(MVG[:, b, :], STG[:, b, :]))
                need(n)
                v.tensor_scalar(VEG[:, c], MVG[:, c, 1], GN_EPS, None, ALU.add).then_inc(s_vg, 1)
                if half:
                    dve.wait_ge(s_rg, 1)
                    v.scalar_tensor_tensor(NBG[:, 0:4], MVG[:, 0:4, 0], -1.0, RSG[:, 0:4], ALU.mult, ALU.mult).then_inc(s_nb, 1)
            dve.wait_ge(s_rg, 2)
            v.scalar_tensor_tensor(NBG[:, 4:8], MVG[:, 4:8, 0], -1.0, RSG[:, 4:8], ALU.mult, ALU.mult).then_inc(s_nb, 1)
            dve.wait_ge(ld["gb"], 32)
            dve.wait_ge(s_const, 1)
            for i in range(STEPS):
                a, b, r, k, s = (j if 0 <= j < B else None for j in (i, i - 1, i - 3, i - 4, i - 5))
                if r is not None:
                    dve.wait_ge(s_lg, r + 1)
                    v.tensor_reduce(NM[:], PS[:, LOGIT, 0:E], AX.X, ALU.max, negate=True).then_inc(s_nm, 1)
                if k is not None:
                    dve.wait_ge(s_rk, k + 1)
                    sel = tick(v.tensor_tensor(SEL[:], OH[:, k % 2, :, :],
                                               PS[:, RANK, 0:E].unsqueeze(1).to_broadcast([128, TOPK, E]), ALU.mult))
                if a is not None:
                    dve.wait_ge(s_yn, a + 1)
                    y0 = tick(v.tensor_tensor(Y0[:], YN[:, a, :], GAM[:], ALU.mult))
                if k is not None:
                    need(sel)
                    rk = tick(v.tensor_reduce(RK[:], SEL[:], AX.X, ALU.add))
                if a is not None:
                    need(y0)
                    y1 = tick(v.tensor_tensor(Y1[:], Y0[:], BET[:], ALU.add))
                if k is not None:
                    need(rk)
                    v.scalar_tensor_tensor(SLOT[:, k, :], RK[:], float(E), IDF[:, k % 2, 0:TOPK],
                                           ALU.mult, ALU.add).then_inc(s_slot, 1)
                if a is not None:
                    need(y1)
                    dve.wait_ge(s_wrc, a // 2 + 1)
                    ge(dve, s_zt, a - 1)
                    v.tensor_tensor(Z[:, a % 2, :], Y1[:], WR[:, a, :], ALU.mult).then_inc(s_z, 1)
                if b is not None:
                    dve.wait_ge(s_wo, b + 1)
                    v.tensor_tensor(X[:, b, :], PS[:, WO, 0:D], X[:, b, :], ALU.add).then_inc(s_x2, 1)
                if r is not None:
                    dve.wait_ge(s_ex, r + 1)
                    top = tick(v.max(TOP[:], EX[:]))
                if b is not None:
                    dve.wait_ge(s_x2, b + 1)
                    st = tick(v.bn_stats(ST2[:], X[:, b, :]))
                if r is not None:
                    need(top)
                    ts = tick(v.tensor_reduce(TS[:], TOP[:, 0:TOPK], AX.X, ALU.add))
                    idx = tick(v.max_index(IDX[:], TOP[:], EX[:]))
                if b is not None:
                    need(st)
                    mv = tick(v.bn_aggr(MV2[:], ST2[:]))
                if r is not None:
                    need(idx)
                    idf = tick(v.tensor_copy(IDF[:, r % 2, :], IDX[:]))
                    td = tick(v.scalar_tensor_tensor(TD[:], ZS[:], TOP_EPS, TS[:], ALU.mult, ALU.add))
                if b is not None:
                    need(mv)
                    v.tensor_scalar(VE2[:], MV2[:, 1:2], LN_EPS, None, ALU.add).then_inc(s_v2, 1)
                if r is not None:
                    need(td)
                    oh = tick(v.tensor_tensor(OH[:, r % 2, :, :], IOE[:].unsqueeze(1).to_broadcast([128, TOPK, E]),
                                              IDF[:, r % 2, 0:TOPK].unsqueeze(2).to_broadcast([128, TOPK, E]), ALU.is_equal))
                    rt = tick(v.reciprocal(RT[:], TD[:]))
                    need(oh)
                    ge(dve, s_rk, r - 1)
                    m = tick(v.tensor_reduce(M[:, r % 2, :], OH[:, r % 2, :, :].rearrange("p j e -> p e j"), AX.X, ALU.add))
                    need(rt)
                    v.tensor_scalar(PAY[:, r, :, 1].bitcast(f32), TOP[:, 0:TOPK], RT[:, 0:1], None, ALU.mult)
                    need(m)
                    v.tensor_tensor(MS[:, r + 1, :], MS[:, r, :], M[:, r % 2, :], ALU.add).then_inc(s_m, 1)
                if b is not None:
                    dve.wait_ge(s_r2, b + 1)
                    v.tensor_scalar(HN[:, b, :], X[:, b, :], MV2[:, 0:1], RS2[:, 0:1],
                                    ALU.subtract, ALU.mult).then_inc(s_h, 1)
                if s is not None:
                    dve.wait_ge(s_sex, s + 1)
                    link(v.scalar_tensor_tensor(SSG[:], SEX[:], 1.0, PS[:, GATE, 0:SF], ALU.add, ALU.mult))
                    ge(dve, s_st, s)
                    v.scalar_tensor_tensor(SAC[:], SSG[:], 0.5, PS[:, UP, 0:SF], ALU.mult, ALU.mult).then_inc(s_sact, 1)
            dve.wait_ge(s_cnt, 1)
            link(v.tensor_tensor(OVF[:].rearrange("p (k e) -> p k e", e=E),
                                 PS[:, WO, 0:E].unsqueeze(1).to_broadcast([128, MAXE - 1, E]),
                                 THR[:].rearrange("p (k e) -> p k e", e=E), ALU.is_gt))
            link(v.tensor_tensor_scan(PRE[:], OVF[:], ZERO[:, 0:COLS], 0.0, ALU.add, ALU.add))
            link(v.tensor_scalar(LE[:], PRE[:], PM64[:, 0:1], 0.0, ALU.is_le, ALU.add, accum_out=CNT[:, 0:1]))
            link(v.tensor_tensor(CNT[:], CNT[:], PMIN[:], ALU.add))
            link(v.tensor_copy(LST[:, 0:1], CNT[:]))
            v.tensor_scalar(TT[:], PRE[0:1, COLS - 1:COLS], float(E), None, ALU.add)
            v.tensor_scalar(LST[:, 1:2], LST[:, 0:1], E - 1, None, ALU.bitwise_and).then_inc(s_list, 1)

            def entries(t, w, col):
                v.tensor_copy(IDR[:, w % U, :], TBL[:, bass.ds(col * 2, 2)] if not isinstance(col, int)
                              else TBL[:, 2 * col:2 * col + 2]).then_inc(s_id, 1)

            def hidden(t, w):
                ge(dve, s_sg, t + (w + 1))
                ge(dve, s_at, t + (w - 1))
                v.scalar_tensor_tensor(AC[:, w % 2, :], SG[:, w % 2, :], IDR[:, w % U, 1:2].bitcast(f32),
                                       PS[:, 2 + w % 2, F:2 * F], ALU.mult, ALU.mult).then_inc(s_act, 1)

            def step(i, u, listed):
                t = i * U
                ge(dve, s_at, t + (u + 1))
                ge(dve, s_d, t + (u - 1))
                v.tensor_copy(ATT[:, u % 2, :, :],
                              PS[0:FC, 4 + u % 2, 0:256].rearrange("p (c n) -> p c n", c=2)).then_inc(s_atc, 1)
                hidden(t, u + 1)
                w = u + LOOK_ID
                ge(dve, s_acc[(w - U) % 2], i * (16 * U // 2) + 16 * ((w - U) // 2 + 1))
                if listed:
                    col = dve.value_load(LROW[0:1, bass.ds(i * (2 * U) + 2 * w, 1)], min_val=0, max_val=BLK * E - 1)
                else:
                    col = t + w
                entries(t, w, col)

            dve.wait_ge(s_tbl, 16)
            for w in range(LOOK_ID):
                entries(0, w, w)
            dve.wait_ge(s_id, LOOK_ID)
            hidden(0, 0)
            dve.wait_ge(s_list, 1)
            T = dve.value_load(TT[0:1, 0:1], min_val=E, max_val=TILES - 1)
            for u in range(U):
                step(0, u, False)
            with dve.Fori(1, E // U - 1) as i:
                for u in range(U):
                    step(i, u, False)
            dve.wait_ge(s_lrow, 16)
            with dve.Fori(E // U - 1, TILES // U) as i:
                for u in range(U):
                    with dve.If(i * U + u < T):
                        step(i, u, True)

        @block.tensor
        def _(pe):
            mm, tr = nc.tensor.matmul, nc.tensor.transpose
            def x_rows(g):
                pe.wait_ge(s_xn, 2 * g + 2)
                if g >= 2:
                    pe.wait_ge(s_ktc, g - 1)
                for k in range(KD):
                    for b in range(2):
                        last = tr(PS[:, g, (k * 2 + b) * 128:(k * 2 + b + 1) * 128],
                                  XN[:, 2 * g + b, k * 128:(k + 1) * 128], IDN)
                last.then_inc(s_xt, 1)

            def q(j):
                pe.wait_ge(s_xtc, 2 * (j // 2) + 2)
                mm(PS[:, 4 + j, :], WH[:, j % 2, :], XNT[:, j % 2, (j // 2) * HALF:(j // 2 + 1) * HALF],
                   start=True, stop=True).then_inc(s_q, 1)

            def gate(g):
                for b in (2 * g, 2 * g + 1):
                    for k in range(KD):
                        last = mm(PS[:, W_BANK[g], (b % 2) * D:(b % 2 + 1) * D], XNT[:, k, b * S:(b + 1) * S],
                                  WGT[:, k, :], start=(k == 0), stop=(k == KD - 1))
                last.then_inc(s_wr, 1)

            def attend(half):
                for h in range(H):
                    last = mm(PS[:, 4 + 2 * half + h, :], AT[:, h, :],
                              V[:, h, 4 * half:4 * half + 4, :].rearrange("p b e -> p (b e)"), start=True, stop=True)
                last.then_inc(s_o, 1)

            pe.wait_ge(ld["cst"], 16)
            x_rows(0)
            x_rows(1)
            pe.wait_ge(ld["wh"], 16)
            q(0)
            q(1)
            pe.wait_ge(ld["ctx"], 16)
            for j in range(4):
                mm(PS[:, K_BANK[j], :], WH[:, j % 2, :], CT[:, j % 2, (j // 2) * HALF:(j // 2 + 1) * HALF],
                   start=True, stop=True).then_inc(s_kt, 1)
            x_rows(2)
            x_rows(3)
            q(2)
            q(3)
            for g in range(4):
                pe.wait_ge(s_ktc, 2 * (g // 2) + 2)
                if g < 2:
                    pe.wait_ge(s_qc, g + 1)
                else:
                    pe.wait_ge(s_ktc, g + 1)
                for h in range(H):
                    for b in range(2):
                        last = tr(PS[:, V_BANK[g], (h * 2 + b) * 128:(h * 2 + b + 1) * 128],
                                  KT[:, h, (2 * g + b) * S:(2 * g + b + 1) * S], IDN)
                last.then_inc(s_v, 1)
            pe.wait_ge(s_qc, 4)
            for h in range(H):
                for b in range(B):
                    last = mm(PS[:, SCORE, h * S:(h + 1) * S], KT[:, h, b * S:(b + 1) * S], QT[:, h, b * S:(b + 1) * S],
                              start=(b == 0), stop=(b == B - 1))
            last.then_inc(s_sc, 1)
            pe.wait_ge(ld["wg"], 16)
            gate(0)
            pe.wait_ge(s_a, 1)
            pe.wait_ge(s_vc, 4)
            attend(0)
            attend(1)
            gate(1)
            gate(2)
            pe.wait_ge(s_wrc, 1)
            gate(3)
            for n in ("wo", "gw", "wsg", "wsd"):
                pe.wait_ge(ld[n], 16)
            pe.wait_ge(s_const, 1)
            for i in range(STEPS):
                if 0 <= i - 3 < B:
                    r = i - 3
                    pe.wait_ge(s_htc, r + 1)
                    ge(pe, s_ex, r)
                    if r == 0:
                        pe.wait_ge(s_yn, B)
                    for k in range(KD):
                        last = mm(PS[:, LOGIT, 0:E], HT[:, k, r * S:(r + 1) * S], GWT[:, k, :],
                                  start=(k == 0), stop=(k == KD - 1))
                    last.then_inc(s_lg, 1)
                if 0 <= i - 4 < B:
                    k = i - 4
                    if k == 0:
                        pe.wait_ge(s_wrc, 4)
                    pe.wait_ge(s_m, k + 1)
                    ge(pe, s_slot, k)
                    mm(PS[:, RANK, 0:E], TRI, M[:, k % 2, :], start=True, stop=False)
                    mm(PS[:, RANK, 0:E], ONE[:], MS[:, k, :], start=False, stop=True).then_inc(s_rk, 1)
                if 0 <= i - 1 < B:
                    b = i - 1
                    pe.wait_ge(s_ztc, b + 1)
                    ge(pe, s_x2, b)
                    for k in range(KD):
                        last = mm(PS[:, WO, 0:D], ZT[:, b % 2, k, :], WOT[:, k, :], start=(k == 0), stop=(k == KD - 1))
                    last.then_inc(s_wo, 1)
                if 0 <= i - 5 < B:
                    s = i - 5
                    ge(pe, s_sact, s)
                    for g in range(2):
                        for k in range(KD):
                            last = mm(PS[:, GATE + g, 0:SF], HT[:, k, s * S:(s + 1) * S], WSG[:, k, g * SF:(g + 1) * SF],
                                      start=(k == 0), stop=(k == KD - 1))
                    last.then_inc(s_sgu, 1)
                if i < B:
                    if i == 0:
                        pe.wait_ge(s_wrc, 4)
                    pe.wait_ge(s_z, i + 1)
                    ge(pe, s_htc, i - 2)
                    for k in range(KD):
                        last = tr(PS[:, ZH, k * 128:(k + 1) * 128], Z[:, i % 2, k * 128:(k + 1) * 128], IDN)
                    last.then_inc(s_zt, 1)
                if 0 <= i - 6 < B:
                    s = i - 6
                    pe.wait_ge(s_sact, s + 1)
                    ge(pe, s_stc, s)
                    for c in range(SF // FC):
                        last = tr(PS[0:FC, STB, c * 128:(c + 1) * 128], SAC[:, c * FC:(c + 1) * FC], IDN)
                    last.then_inc(s_st, 1)
                if 0 <= i - 2 < B:
                    r = i - 2
                    pe.wait_ge(s_h, r + 1)
                    ge(pe, s_ztc, min(i + 1, B))
                    for k in range(KD):
                        last = tr(PS[:, ZH, 256 + k * 128:256 + (k + 1) * 128], HN[:, r, k * 128:(k + 1) * 128], IDN)
                    last.then_inc(s_ht, 1)
                if 0 <= i - 7 < B:
                    s = i - 7
                    pe.wait_ge(s_stc, s + 1)
                    ge(pe, s_shc, s)
                    for c in range(SF // FC):
                        last = mm(PS[:, SDB, 0:D], SACT[:, c, :], WSD[:, c, :], start=(c == 0), stop=(c == SF // FC - 1))
                    last.then_inc(s_sd, 1)
            mm(PS[:, WO, 0:E], ONE[:], MS[:, B, :], start=True, stop=True).then_inc(s_cnt, 1)

            def rows(t, w):
                g = w % LOOK_G
                for k in range(KD):
                    last = tr(PS[:, w % 2, k * 128:(k + 1) * 128], XG[:, g, k * 128:(k + 1) * 128], IDN)
                last.then_inc(s_xg, 1)

            def gate_up(t, w, slot):
                for k in range(KD):
                    rhs = (WGU[:, slot * 2 * SF + k * SF:slot * 2 * SF + (k + 1) * SF] if isinstance(slot, int)
                           else WGU[:, bass.ds(slot * (2 * SF) + k * SF, SF)])
                    last = mm(PS[:, 2 + w % 2, 0:SF], XT[:, w % 2, k, :], rhs, start=(k == 0), stop=(k == KD - 1))
                last.then_inc(s_gu, 1)

            def step(i, u):
                t = i * U
                pe.wait_ge(s_act, t + (u + 1))
                ge(pe, s_atc, t + (u - 1))
                for c in range(2):
                    last = tr(PS[0:FC, 4 + u % 2, c * 128:(c + 1) * 128], AC[:, u % 2, c * FC:(c + 1) * FC], IDN)
                last.then_inc(s_at, 1)
                w = u + 1
                pe.wait_ge(s_xgc, t + (w + 1))
                pe.wait_ge(s_w[w % U], i * 32 + 32 * (w // U + 1))
                pe.wait_ge(s_act, t + w)
                gate_up(t, w, (i * U + w) % R)
                pe.wait_ge(s_atc, t + (u + 1))
                ge(pe, s_y, t + (u - 1))
                slot = (i * U + u) % R
                for c in range(2):
                    rhs = (WDN[:, slot * 2 * D + c * D:slot * 2 * D + (c + 1) * D] if isinstance(slot, int)
                           else WDN[:, bass.ds(slot * (2 * D) + c * D, D)])
                    last = mm(PS[:, 6 + u % 2, 0:D], ATT[:, u % 2, c, :], rhs, start=(c == 0), stop=(c == 1))
                last.then_inc(s_d, 1)
                w = u + LOOK_R
                pe.wait_ge(s_g[w % LOOK_G], i * (16 * U // LOOK_G) + 16 * (w // LOOK_G + 1))
                pe.wait_ge(s_xgc, t + (w - 1))
                rows(t, w)

            pe.wait_ge(s_list, 1)
            for w in range(2):
                pe.wait_ge(s_g[w], 16)
                rows(0, w)
            pe.wait_ge(s_xgc, 1)
            pe.wait_ge(s_w[0], 32)
            gate_up(0, 0, 0)
            pe.wait_ge(s_g[2], 16)
            rows(0, 2)
            T = pe.value_load(TT[0:1, 0:1], min_val=E, max_val=TILES - 1)
            for u in range(U):
                step(0, u)
            with pe.Fori(1, E // U - 1) as i:
                for u in range(U):
                    step(i, u)
            with pe.Fori(E // U - 1, TILES // U) as i:
                for u in range(U):
                    with pe.If(i * U + u < T):
                        step(i, u)


def shape_constants():
    f = np.float32
    gam = (1.0 - 2.0 ** (-5.0 - np.arange(H, dtype=f))).astype(f)
    idx = np.arange(S, dtype=f)
    expo = idx[None, :] - idx[:, None]
    d = np.where(expo[None] <= 0, gam[:, None, None] ** expo[None], f(0)).astype(f)
    d = (d / np.sqrt(d.sum(axis=-1, dtype=f))[:, None, :]).astype(f)
    mask_t = d.transpose(2, 0, 1).reshape(S, H * S)
    tri = np.triu(np.ones((128, 128), f), 1)
    return np.ascontiguousarray(np.concatenate([np.eye(128, dtype=f), tri, mask_t], axis=1), dtype=f)


def kernel(**inputs):
    import concourse.bacc as bacc
    from concourse.bass_utils import run_bass_kernel_spmd

    a = {k: np.asarray(v) for k, v in inputs.items()}
    chunk = lambda w, p: w.reshape(-1, p, w.shape[-1]).transpose(1, 0, 2)
    arrays = {
        "x": a["x"].transpose(1, 0, 2),
        "ctxT": a["ctx_2048"].reshape(N, H, HD).transpose(2, 1, 0),
        "Wh": a["L0_xattn_Wh"].transpose(1, 0, 2),
        "wg": chunk(a["L0_xattn_wg_w"], 128),
        "wo": chunk(a["L0_xattn_wo_w"], 128),
        "gam": np.broadcast_to(a["L0_xattn_gn_gamma"], (128, D)),
        "bet": np.broadcast_to(a["L0_xattn_gn_beta"], (128, D)),
        "gw": chunk(a["L0_ffn_gate_w"].T, 128),
        "wgu": a["L0_ffn_w_gate_up"].reshape(E, SF, KD, 128).transpose(0, 3, 2, 1).reshape(E, 128, KD * SF),
        "wdn": a["L0_ffn_w_down"].reshape(E, D, 2, FC).transpose(0, 3, 2, 1).reshape(E, FC, 2 * D),
        "wsg": chunk(a["L0_ffn_ws_gate_up"].T, 128),
        "wsd": chunk(a["L0_ffn_ws_down"].T, FC),
        "cst": shape_constants(),
    }
    arrays = {k: np.ascontiguousarray(v) for k, v in arrays.items()}
    nc = bacc.Bacc("TRN2", target_bir_lowering=False, num_devices=1)
    f32 = mybir.dt.float32
    args = [nc.dram_tensor("in_" + k, v.shape, f32, kind="ExternalInput").ap() for k, v in arrays.items()]
    out = nc.dram_tensor("out_rows", (N + 128, D), f32, kind="ExternalOutput").ap()
    program(nc, *args, out)
    r = run_bass_kernel_spmd(nc, [{"in_" + k: v for k, v in arrays.items()}], core_ids=[0])
    return np.asarray(r.results[0]["out_rows"])[:N].reshape(B, S, D)
```

```python
import numpy as np
import concourse.bass as bass
from concourse import mybir
from contextlib import ExitStack

B, S, D = 8, 128, 256
N = B * S
H, HD = 2, 128
KD = D // 128
E, F, TOPK = 64, 176, 6
SF = 2 * F
FC = 88
LN_EPS, GN_EPS, TOP_EPS = 1e-5, 1e-3, 1e-20
MAXE = N // 128
BLK = MAXE + 1
COLS = (MAXE - 1) * E
EXTRA = (N * TOPK) // 128
TILES = E + EXTRA
R = 16
U = R
GRP = 8
LOOK_ID, LOOK_G, LOOK_R = 6, 5, 3
XR = 4
STEPS = B + 5
P_BANK, V_BANK, SCORE = (2, 3, 6, 7), (4, 5, 0, 2), (3, 6)
X_BANK, W_BANK = (0, 1, 0, 1), (0, 3, 0, 3)
HALF = 4 * S


def program(nc, x, ctxT, Wh, wg, wo, gam, bet, gw, wgu, wdn, wsg, wsd, cst, out):
    f32, f32r, i32, u32 = mybir.dt.float32, mybir.dt.float32r, mybir.dt.int32, mybir.dt.uint32
    ALU, ACT, AX = mybir.AluOpType, mybir.ActivationFunctionType, mybir.AxisListType

    tbl = nc.dram_tensor("slot_table", [BLK * 128, E, 2], i32).ap()
    hbuf = nc.dram_tensor("h_rows", [N + 128, D], f32).ap()
    acc1 = nc.dram_tensor("acc_odd", [N + 128, D], f32).ap()
    lst_d = nc.dram_tensor("tile_list", [128, 2], i32).ap()

    with ExitStack() as ctx:
        def sb(name, shape, dt=f32):
            return ctx.enter_context(nc.sbuf_tensor(name, shape, dt))

        def sem(name):
            return ctx.enter_context(nc.semaphore(name))

        X = sb("X", [128, B, D])
        CT = sb("CT", [128, H, N])
        XN = sb("XN", [128, B, D])
        XNT = sb("XNT", [128, KD, N])
        PT = sb("PT", [128, H, N])
        HN = sb("HN", [128, B, D])
        V = sb("V", [128, H, B, HD])
        HT = CT
        WR = XN[:, :, :].rearrange("p b d -> p (b d)").rearrange("p (k n) -> p k n", k=KD)
        SH = XNT[:, :, :].rearrange("p k n -> p (k n)").rearrange("p (b d) -> p b d", b=B)
        YN = PT[:, :, :].rearrange("p h n -> p (h n)").rearrange("p (b d) -> p b d", b=B)
        WH = sb("WH", [128, H, HD])
        WHT = sb("WHT", [128, H, HD])
        WW = sb("WW", [128, H, HD])
        WGT = sb("WGT", [128, KD, D])
        WOT = sb("WOT", [128, KD, D])
        GWT = sb("GWT", [128, KD, E])
        WSG = sb("WSG", [128, KD, 2 * SF])
        WSD = sb("WSD", [FC, SF // FC, D])
        GAM = sb("GAM", [128, KD])
        BET = sb("BET", [128, KD])
        CST = sb("CST", [128, 512])
        IDN, TRI, MASK = CST[:, 0:128], CST[:, 128:256], CST[:, 256:512]
        ONE = sb("ONE", [128, 128])
        IOE = sb("IOE", [128, E])
        THR = sb("THR", [128, COLS])
        PM64 = sb("PM64", [128, 1])
        PMIN = sb("PMIN", [128, 1])
        ZERO = sb("ZERO", [128, 512])
        INIT = sb("INIT", [128, E, 2], i32)
        PAY = sb("PAY", [128, B, TOPK, 2], i32)
        SLOT = sb("SLOT", [128, B, TOPK], i32)
        AT = sb("AT", [128, H, S])
        AT0 = sb("AT0", [128, H, S])
        AT1 = sb("AT1", [128, H, S])
        NHALF = sb("NHALF", [128, 1])
        ST1 = sb("ST1", [128, B, 6])
        MV1 = sb("MV1", [128, B, 2])
        RS1 = sb("RS1", [128, B])
        STG = sb("STG", [128, B, 6])
        MVG = sb("MVG", [128, B, 2])
        VE1 = sb("VE1", [128, B])
        VEG = sb("VEG", [128, B])
        VE2 = sb("VE2", [128, 1])
        RSG = sb("RSG", [128, B])
        NBG = sb("NBG", [128, B])
        ST2 = sb("ST2", [128, 6])
        MV2 = sb("MV2", [128, 2])
        RS2 = sb("RS2", [128, 1])
        ZG = sb("ZG", [128, 2, KD, 128])
        ZT = sb("ZT", [128, 2, KD, 128])
        NM = sb("NM", [128, 1])
        EX = sb("EX", [128, E])
        ZS = sb("ZS", [128, 1])
        TOP = sb("TOP", [128, 8])
        IDX = sb("IDX", [128, 8], u32)
        IDF = sb("IDF", [128, 2, 8])
        TS = sb("TS", [128, 1])
        TD = sb("TD", [128, 1])
        RT = sb("RT", [128, 1])
        OH = sb("OH", [128, 2, TOPK, E])
        SEL = sb("SEL", [128, TOPK, E])
        RK = sb("RK", [128, TOPK])
        M = sb("M", [128, 2, E])
        MS = sb("MS", [128, B + 1, E])
        WARM = sb("WARM", [128, 1])
        SEX = sb("SEX", [128, SF])
        SSG = sb("SSG", [128, SF])
        SAC = sb("SAC", [128, SF])
        SACT = sb("SACT", [FC, SF // FC, 128])
        OVF = sb("OVF", [128, COLS])
        PRE = sb("PRE", [128, COLS])
        LE = sb("LE", [128, COLS])
        CNT = sb("CNT", [128, 1])
        LST = sb("LST", [128, 2], i32)
        TT = sb("TT", [1, 1], i32)
        LROW = sb("LROW", [1, 256], i32)
        TBL = V[:, :, :, :].rearrange("p h b e -> p (h b e)")[:, 0:BLK * E * 2].bitcast(i32)
        IDR = sb("IDR", [128, U, 2], i32)
        XG, YS = YN[:, 0:XR, :], YN[:, XR:XR + 4, :]
        XTH = sb("XTH", [128, 2, KD, 128], f32r)
        XTL = sb("XTL", [128, 2, KD, 128], f32r)
        WGH = sb("WGH", [128, 2, 2 * SF], f32r)
        WGL = sb("WGL", [128, 2, 2 * SF], f32r)
        SG = sb("SG", [128, 2, F])
        AC = sb("AC", [128, 2, F])
        ATT = sb("ATT", [FC, 2, 2, 128])
        WGU = sb("WGU", [128, R * 2 * SF])
        WDN = sb("WDN", [FC, R * 2 * D])
        RANK, ZB, WO, STB, LOGIT, GATE, UP, SDB = range(8)
        PS = ctx.enter_context(nc.psum_tensor("PS", [128, 8, 512], f32))

        ld = {n: sem("ld_" + n) for n in ("ctx0", "ctx1", "wh", "x0", "x1", "idn", "cst", "wg", "wo", "gb", "gw", "wsg", "wsd")}
        s_const, s_init = sem("s_const"), sem("s_init")
        s_wt, s_wtc, s_ww, s_wwc, s_p, s_pc, s_v, s_vc, s_xn, s_xt, s_xta, s_xtd = (
            sem(n) for n in ("s_wt", "s_wtc", "s_ww", "s_wwc", "s_p", "s_pc", "s_v", "s_vc", "s_xn", "s_xt", "s_xta", "s_xtd"))
        s_sc, s_a, s_wr, s_wrc, s_o = (sem(n) for n in ("s_sc", "s_a", "s_wr", "s_wrc", "s_o"))
        s_zt, s_zg, s_z, s_wo, s_x2, s_h, s_ht, s_htc = (
            sem(n) for n in ("s_zt", "s_zg", "s_z", "s_wo", "s_x2", "s_h", "s_ht", "s_htc"))
        s_lg, s_nm, s_ex, s_m, s_rk, s_slot = (sem(n) for n in ("s_lg", "s_nm", "s_ex", "s_m", "s_rk", "s_slot"))
        s_sgu, s_sex, s_sact, s_st, s_stc, s_sd, s_shc = (
            sem(n) for n in ("s_sgu", "s_sex", "s_sact", "s_st", "s_stc", "s_sd", "s_shc"))
        s_v1, s_r1, s_vg, s_rg, s_nb, s_yn, s_v2, s_r2 = (
            sem(n) for n in ("s_v1", "s_r1", "s_vg", "s_rg", "s_nb", "s_yn", "s_v2", "s_r2"))
        s_cnt, s_list, s_lstd, s_lrow = sem("s_cnt"), sem("s_list"), sem("s_lstd"), sem("s_lrow")
        s_tsc, s_tbl, s_tbl_more, s_hst, s_ost = sem("s_tsc"), sem("s_tbl"), sem("s_tbl_more"), sem("s_hst"), sem("s_ost")
        s_dve = sem("s_dve")
        s_w = [sem(f"s_w{u}") for u in range(GRP)]
        s_g = [sem(f"s_g{u}") for u in range(XR)]
        s_acc = [sem(f"s_acc{u}") for u in range(2)]
        s_id, s_xg, s_xgc, s_gu, s_sg, s_act, s_at, s_atc, s_d, s_y = (
            sem(n) for n in ("m_id", "m_xt", "m_xtc", "m_gu", "m_sg", "m_act", "m_at", "m_atc", "m_d", "m_y"))
        s_xl, s_wh, s_wl = sem("m_xl"), sem("m_wh"), sem("m_wl")
        s_fin, s_turn, s_sp = sem("s_fin"), sem("s_turn"), sem("s_sp")
        s_more = [sem(n) for n in ("more_sp", "more_pool", "more_act", "more_dve", "more_pe")]

        block = ctx.enter_context(nc.Block())

        def ge(eng, s, v):
            if not isinstance(v, int) or v > 0:
                eng.wait_ge(s, v)

        def heads_of(b):
            return PS[:, 4 + b // 2, (b % 2) * D:(b % 2 + 1) * D]

        @block.sync
        def _(sp):
            def x_in(half):
                sp.dma_start(X[:, 4 * half:4 * half + 4, :], x[:, 4 * half:4 * half + 4, :]).then_inc(ld[f"x{half}"], 16)

            def ctx_in(half):
                cols = slice(half * HALF, (half + 1) * HALF)
                sp.dma_start(CT[:, :, cols], ctxT[:, :, cols]).then_inc(ld[f"ctx{half}"], 16)

            sp.dma_start(WH[:], Wh).then_inc(ld["wh"], 16)
            sp.dma_start(IDN, cst[:, 0:128]).then_inc(ld["idn"], 16)
            ctx_in(0)
            x_in(0)
            x_in(1)
            ctx_in(1)
            sp.dma_start(CST[:, 128:512], cst[:, 128:512]).then_inc(ld["cst"], 16)
            sp.dma_start(WGT[:], wg).then_inc(ld["wg"], 16)
            sp.dma_start(WOT[:], wo).then_inc(ld["wo"], 16)
            sp.dma_start(GAM[:], gam).then_inc(ld["gb"], 16)
            sp.dma_start(BET[:], bet).then_inc(ld["gb"], 16)
            sp.dma_start(GWT[:], gw).then_inc(ld["gw"], 16)
            sp.dma_start(WSG[:], wsg).then_inc(ld["wsg"], 16)
            sp.dma_start(WSD[:], wsd).then_inc(ld["wsd"], 16)
            sp.wait_ge(s_const, 1)
            blocks = "(k p) e c -> p k (e c)"
            sp.dma_start(tbl.rearrange(blocks, p=128),
                         INIT[:].rearrange("p e c -> p (e c)").unsqueeze(1).to_broadcast([128, BLK, 2 * E])).then_inc(s_init, 16)
            sp.dma_start(acc1[N:N + 128, :], ZERO[:, 0:D]).then_inc(s_init, 16)
            sp.dma_start(hbuf[N:N + 128, :], ZERO[:, 0:D]).then_inc(s_init, 16)
            sp.dma_start(out[N:N + 128, :], ZERO[:, 0:D]).then_inc(s_init, 16)

            def shared_out(s):
                sp.wait_ge(s_shc, s + 1)
                sp.dma_start(acc1[s * S:(s + 1) * S, :], SH[:, s, :]).then_inc(s_ost, 16)

            def load(u, e):
                gu, dn = ((wgu[e], wdn[e]) if isinstance(e, int) else
                          (wgu[bass.ds(e, 1)].rearrange("o p n -> (o p) n"), wdn[bass.ds(e, 1)].rearrange("o p n -> (o p) n")))
                sp.dma_start(WGU[:, u * 2 * SF:(u + 1) * 2 * SF], gu).then_inc(s_w[u % GRP], 16)
                sp.dma_start(WDN[:, u * 2 * D:(u + 1) * 2 * D], dn).then_inc(s_w[u % GRP], 16)

            def load_next(i, u, e):
                sp.wait_ge(s_d, i * U + (u - R + 1))
                sp.sem_inc(s_sp)
                sp.wait_ge(s_w[u % GRP], i * (32 * U // GRP) + 32 * (u // GRP))
                sp.sem_inc(s_sp)
                load(u, e)

            for t in range(R):
                ge(sp, s_w[t % GRP], 32 * (t // GRP))
                load(t, t)
            for i in range(B + 2):
                if i < B:
                    sp.wait_ge(s_x2, i + 1)
                    sp.dma_start(out[i * S:(i + 1) * S, :], X[:, i, :]).then_inc(s_ost, 16)
                    sp.wait_ge(s_h, i + 1)
                    sp.dma_start(hbuf[i * S:(i + 1) * S, :], HN[:, i, :]).then_inc(s_hst, 16)
                if i >= 5:
                    shared_out(i - 5)
            sp.wait_ge(s_list, 1)
            sp.dma_start(lst_d, LST[:]).then_inc(s_lstd, 16)
            shared_out(B - 3)
            sp.wait_ge(s_tsc, 16 * TOPK * B)
            sp.dma_start(TBL[:, 0:2 * E], tbl[0:128].rearrange("p e c -> p (e c)")).then_inc(s_tbl, 16)
            sp.wait_ge(s_g[0], 16)
            for s in range(B - 2, B):
                shared_out(s)
            sp.wait_ge(s_g[XR - 1], 16)
            sp.dma_start(TBL[:, 2 * E:].rearrange("p (k n) -> p k n", k=BLK - 1),
                         tbl[128:].rearrange("(k p) e c -> p k (e c)", p=128)).then_inc(s_tbl_more, 16)
            sp.wait_ge(s_lstd, 16)
            sp.dma_start(LROW[:], lst_d.rearrange("(o t) c -> o (t c)", o=1)).then_inc(s_lrow, 16)
            T = sp.value_load(TT[0:1, 0:1], min_val=E, max_val=TILES - 1)
            sp.wait_ge(s_lrow, 16)
            with sp.Fori(1, E // U) as i:
                for u in range(U):
                    load_next(i, u, i * U + u)
            with sp.Fori(E // U, TILES // U + 1) as i:
                for g in range(0, U, GRP):
                    with sp.If(i * U + (g - 3) < T):
                        for u in range(g, g + GRP):
                            with sp.If(i * U + (u - 3) < T):
                                e = sp.value_load(LROW[0:1, bass.ds(i * (2 * U) + (2 * u + 1), 1)], min_val=0, max_val=E - 1)
                                load_next(i, u, e)
                        sp.sem_inc(s_more[0])

        @block.gpsimd
        def _(pool):
            nc.gpsimd.memset(INIT[:], 0).then_inc(s_init, 1)
            pool.wait_ge(s_init, 1)
            nc.gpsimd.memset(ZERO[:], 0.0).then_inc(s_init, 1)
            nc.gpsimd.iota(INIT[:, :, 0], [[0, E]], base=N, channel_multiplier=1)
            nc.gpsimd.memset(ONE[:], 1.0)
            nc.gpsimd.memset(MS[:, 0, :], 0.0)
            nc.gpsimd.memset(NHALF[:], -0.5)
            nc.gpsimd.iota(PAY[:, :, :, 0], [[S, B], [0, TOPK]], base=0, channel_multiplier=1)
            nc.gpsimd.iota(IOE[:], [[1, E]], base=0, channel_multiplier=0, allow_small_or_imprecise_dtypes=True)
            nc.gpsimd.iota(THR[:], [[128, MAXE - 1], [0, E]], base=128, channel_multiplier=0,
                           allow_small_or_imprecise_dtypes=True)
            nc.gpsimd.iota(PM64[:], [[0, 1]], base=-E, channel_multiplier=1,
                           allow_small_or_imprecise_dtypes=True).then_inc(s_init, 1)
            pool.wait_ge(s_init, 3)
            nc.gpsimd.tensor_scalar(PMIN[:], PM64[:], float(E), float(E), ALU.add, ALU.min).then_inc(s_const, 1)
            minus_half = NHALF[:, 0:1].to_broadcast([128, 4])
            for half in range(2):
                c = slice(4 * half, 4 * half + 4)
                pool.wait_ge(s_v1, half + 1)
                nc.gpsimd.tensor_tensor(RS1[:, c], VE1[:, c], minus_half, ALU.pow).then_inc(s_r1, 1)

            def group_scale(g):
                c = slice(2 * g, 2 * g + 2)
                pool.wait_ge(s_vg, g + 1)
                nc.gpsimd.tensor_tensor(RSG[:, c], VEG[:, c], minus_half[:, 0:2], ALU.pow).then_inc(s_rg, 1)

            group_scale(0)
            for i in range(B + 2):
                k = i - 2
                if i < 2:
                    group_scale(1 + i)
                for j in range(TOPK):
                    if j == 2 and i == 2:
                        group_scale(3)
                    if j == 2 and i < B:
                        pool.wait_ge(s_v2, i + 1)
                        ge(pool, s_h, i)
                        nc.gpsimd.tensor_tensor(RS2[:], VE2[:], NHALF[:], ALU.pow).then_inc(s_r2, 1)
                    if k == 0 and j == 0:
                        pool.wait_ge(s_init, 3 + 4 * 16)
                    if 0 <= k:
                        if j == 0:
                            pool.wait_ge(s_slot, k + 1)
                        pool.indirect_dma_start(tbl.rearrange("r e c -> (r e) c"),
                                                bass.IndirectOffsetOnAxis(ap=SLOT[:, k, j:j + 1], axis=0),
                                                PAY[:, k, j, :], None).then_inc(s_tsc, 16)

            def gather(g, idr):
                pool.indirect_dma_start(XG[:, g, :], None, hbuf,
                                        bass.IndirectOffsetOnAxis(ap=IDR[:, idr, 0:1], axis=0)).then_inc(s_g[g], 16)

            def step(i, u):
                t = i * U
                ge(pool, s_id, t + (u + LOOK_G + 1))
                ge(pool, s_xg, t + (u + LOOK_G - XR + 1))
                pool.sem_inc(s_turn)
                gather((u + LOOK_G) % XR, (u + LOOK_G) % U)
                if isinstance(i, int) and u == 0:
                    pool.wait_ge(s_ost, 32 * B)
                ge(pool, s_y, t + (u + 1))
                ge(pool, s_acc[u % 2], i * (16 * U // 2) + 16 * (u // 2))
                pool.sem_inc(s_turn)
                pool.indirect_dma_start((out, acc1)[u % 2],
                                        bass.IndirectOffsetOnAxis(ap=IDR[:, u, 0:1], axis=0),
                                        YS[:, u % 4, :], None, compute_op=ALU.add).then_inc(s_acc[u % 2], 16)

            pool.wait_ge(s_hst, 16 * B)
            for t in range(LOOK_G):
                ge(pool, s_id, t + 1)
                ge(pool, s_xg, t - XR + 1)
                gather(t % XR, t)
            T = pool.value_load(TT[0:1, 0:1], min_val=E, max_val=TILES - 1)
            for u in range(U):
                step(0, u)
            with pool.Fori(1, E // U) as i:
                for u in range(U):
                    step(i, u)
            with pool.Fori(E // U, TILES // U) as i:
                with pool.If(i * U < T):
                    for g in range(0, U, GRP):
                        with pool.If(i * U + g < T):
                            for u in range(g, g + GRP):
                                with pool.If(i * U + u < T):
                                    step(i, u)
                            pool.sem_inc(s_more[1])
                    pool.sem_inc(s_more[1])
            for g in range(XR):
                pool.wait_ge(s_g[g], (T + (LOOK_G + XR - 1 - g)) // XR * 16)
            pool.wait_ge(s_acc[0], (T + 1) // 2 * 16)
            pool.wait_ge(s_acc[1], T // 2 * 16)
            pool.sem_inc(s_turn)
            pool.dma_start(out[0:N, :], acc1[0:N, :], accum_op=ALU.add, max_dma_last_dim=8192).then_inc(s_fin, 16)
            pool.wait_ge(s_fin, 16)

        @block.scalar
        def _(act):
            def product(j):
                act.wait_ge(s_p, j + 1)
                nc.scalar.copy(PT[:, j % 2, (j // 2) * HALF:(j // 2 + 1) * HALF], PS[:, P_BANK[j], :]).then_inc(s_pc, 1)

            def value(g):
                act.wait_ge(s_v, g + 1)
                nc.scalar.copy(V[:, :, 2 * g:2 * g + 2, :],
                               PS[:, V_BANK[g], :].rearrange("p (h b e) -> p h b e", h=H, b=2)).then_inc(s_vc, 1)

            def relu_gate(g):
                act.wait_ge(s_wr, g + 1)
                nc.scalar.activation(WR[:, g % 2, (g // 2) * HALF:(g // 2 + 1) * HALF], PS[:, W_BANK[g], :],
                                     ACT.Relu).then_inc(s_wrc, 1)

            def normalise(b):
                act.wait_ge(s_nb, b // 2 + 1)
                nc.scalar.activation(YN[:, b, :], heads_of(b), ACT.Identity,
                                     bias=NBG[:, b:b + 1], scale=RSG[:, b:b + 1]).then_inc(s_yn, 1)

            def affine(b):
                act.wait_ge(s_zt, b + 1)
                ge(act, s_z, b - 1)
                for k in range(KD):
                    last = nc.scalar.activation(ZG[:, b % 2, k, :], PS[:, ZB, k * 128:(k + 1) * 128], ACT.Identity,
                                                bias=BET[:, k:k + 1], scale=GAM[:, k:k + 1])
                last.then_inc(s_zg, 1)

            act.wait_ge(s_wt, 1)
            nc.scalar.copy(WHT[:], PS[:, 0, 0:256].rearrange("p (h e) -> p h e", h=H)).then_inc(s_wtc, 1)
            act.wait_ge(s_ww, 1)
            nc.scalar.copy(WW[:], PS[:, 1, 0:256].rearrange("p (h e) -> p h e", h=H)).then_inc(s_wwc, 1)
            for j in range(2):
                product(j)
            value(0)
            value(1)
            for j in range(2, 4):
                product(j)
            for g in range(2):
                act.wait_ge(s_xt, g + 1)
                nc.scalar.copy(XNT[:, :, g * 256:(g + 1) * 256],
                               PS[:, X_BANK[g], :].rearrange("p (k n) -> p k n", k=KD)).then_inc(s_xta, 1)
            value(2)
            value(3)
            relu_gate(0)
            normalise(0)
            relu_gate(1)
            act.wait_ge(ld["gb"], 32)
            affine(0)
            normalise(1)
            for i in range(STEPS):
                if 0 <= i - 1 < B:
                    r = i - 1
                    act.wait_ge(s_ht, r + 1)
                    nc.scalar.copy(HT[:, :, r * S:(r + 1) * S],
                                   PS[:, LOGIT, 256:512].rearrange("p (k n) -> p k n", k=KD)).then_inc(s_htc, 1)
                if 0 <= i - 4 < B:
                    s = i - 4
                    act.wait_ge(s_st, s + 1)
                    ge(act, s_sd, s)
                    nc.scalar.copy(SACT[:], PS[0:FC, STB, :].rearrange("p (c n) -> p c n", c=SF // FC)).then_inc(s_stc, 1)
                if 0 <= i - 5 < B:
                    s = i - 5
                    act.wait_ge(s_sd, s + 1)
                    nc.scalar.copy(SH[:, s, :], PS[:, SDB, 0:D]).then_inc(s_shc, 1)
                if 0 <= i - 1 < B:
                    r = i - 1
                    act.wait_ge(s_nm, r + 1)
                    ge(act, s_m, r)
                    nc.scalar.activation(EX[:], PS[:, LOGIT, 0:E], ACT.Exp, bias=NM[:, 0:1],
                                         accum_out=ZS[:, 0:1]).then_inc(s_ex, 1)
                if i + 1 < B:
                    affine(i + 1)
                if 0 <= i - 3 < B:
                    s = i - 3
                    act.wait_ge(s_sgu, s + 1)
                    ge(act, s_sact, s)
                    nc.scalar.activation(SEX[:], PS[:, GATE, 0:SF], ACT.Tanh, scale=0.5).then_inc(s_sex, 1)
                    if s == B - 1:
                        nc.scalar.activation(WARM[:], NHALF[:], ACT.Silu)
                if i == 1:
                    normalise(3)
                if 1 <= i < 3:
                    relu_gate(1 + i)
                if i == 0:
                    normalise(2)
                if i in (2, 3):
                    normalise(2 * i)
                    normalise(2 * i + 1)

            def rows_in(t, v):
                ge(act, s_xg, t + (v + 1))
                ge(act, s_gu, t + (v - 1))
                nc.scalar.copy(XTH[:, v % 2, :, :],
                               PS[:, v % 2, 0:256].rearrange("p (k n) -> p k n", k=KD)).then_inc(s_xgc, 1)

            def weights_high(i, w):
                act.wait_ge(s_w[w % GRP], i * (32 * U // GRP) + 32 * (w // GRP + 1))
                ge(act, s_gu, i * U + (w - 1))
                nc.scalar.copy(WGH[:, w % 2, :], WGU[:, w % R * 2 * SF:(w % R + 1) * 2 * SF]).then_inc(s_wh, 1)

            def silu(t, v):
                ge(act, s_gu, t + (v + 1))
                ge(act, s_act, t + (v - 1))
                nc.scalar.activation(SG[:, v % 2, :], PS[:, 2 + v % 2, 0:F], ACT.Silu).then_inc(s_sg, 1)

            def step(i, u):
                t = i * U
                silu(t, u + 1)
                weights_high(i, u + 3)
                ge(act, s_d, t + (u + 1))
                ge(act, s_acc[u % 2], i * (16 * U // 2) + 16 * (u // 2 - 1))
                nc.scalar.copy(YS[:, u % 4, :], PS[:, 6 + u % 2, 0:D]).then_inc(s_y, 1)
                rows_in(t, u + LOOK_R)

            weights_high(0, 0)
            weights_high(0, 1)
            rows_in(0, 0)
            silu(0, 0)
            weights_high(0, 2)
            rows_in(0, 1)
            rows_in(0, 2)
            act.wait_ge(s_list, 1)
            T = act.value_load(TT[0:1, 0:1], min_val=E, max_val=TILES - 1)
            for u in range(U):
                step(0, u)
            with act.Fori(1, E // U) as i:
                for u in range(U):
                    step(i, u)
            with act.Fori(E // U, TILES // U) as i:
                for g in range(0, U, GRP):
                    with act.If(i * U + g < T):
                        for u in range(g, g + GRP):
                            with act.If(i * U + u < T):
                                step(i, u)
                        act.sem_inc(s_more[2])

        @block.vector
        def _(dve):
            count = [0]

            def tick(ins):
                count[0] += 1
                ins.then_inc(s_dve, 1)
                return count[0]

            def need(n):
                dve.wait_ge(s_dve, n)

            def link(ins):
                need(tick(ins))

            v = nc.vector
            def x_stats(half):
                c = slice(4 * half, 4 * half + 4)
                dve.wait_ge(ld[f"x{half}"], 16)
                for b in range(4 * half, 4 * half + 4):
                    n = tick(v.bn_stats(ST1[:, b, :], X[:, b, :]))
                need(n)
                for b in range(4 * half, 4 * half + 4):
                    n = tick(v.bn_aggr(MV1[:, b, :], ST1[:, b, :]))
                need(n)
                v.tensor_scalar(VE1[:, c], MV1[:, c, 1], LN_EPS, None, ALU.add).then_inc(s_v1, 1)

            x_stats(0)
            x_stats(1)
            for half in range(2):
                dve.wait_ge(s_r1, half + 1)
                for b in range(4 * half, 4 * half + 4):
                    v.tensor_scalar(XN[:, b, :], X[:, b, :], MV1[:, b, 0:1], RS1[:, b:b + 1],
                                    ALU.subtract, ALU.mult).then_inc(s_xn, 1)
            for g in range(2, 4):
                dve.wait_ge(s_xt, g + 1)
                v.tensor_copy(XNT[:, :, g * 256:(g + 1) * 256],
                              PS[:, X_BANK[g], :].rearrange("p (k n) -> p k n", k=KD)).then_inc(s_xtd, 1)
            dve.wait_ge(ld["cst"], 16)
            dve.wait_ge(s_sc, 1)
            link(v.scalar_tensor_tensor(AT0[:], PS[:, SCORE[0]:SCORE[1] + 1:SCORE[1] - SCORE[0], 0:S],
                                        float(np.float32(1.0) / np.sqrt(np.float32(HD))),
                                        MASK.rearrange("p (h s) -> p h s", h=H), ALU.mult, ALU.mult))
            link(v.scalar_tensor_tensor(AT1[:], AT0[:], -1.0, AT0[:], ALU.mult, ALU.max))
            v.tensor_scalar(AT[:], AT1[:], 1.0, None, ALU.max).then_inc(s_a, 1)
            def group_stats(g):
                c = slice(2 * g, 2 * g + 2)
                dve.wait_ge(s_o, g + 1)
                for b in (2 * g, 2 * g + 1):
                    n = tick(v.bn_stats(STG[:, b, :], heads_of(b)))
                need(n)
                for b in (2 * g, 2 * g + 1):
                    n = tick(v.bn_aggr(MVG[:, b, :], STG[:, b, :]))
                need(n)
                v.tensor_scalar(VEG[:, c], MVG[:, c, 1], GN_EPS, None, ALU.add).then_inc(s_vg, 1)

            def group_bias(g):
                c = slice(2 * g, 2 * g + 2)
                dve.wait_ge(s_rg, g + 1)
                v.scalar_tensor_tensor(NBG[:, c], MVG[:, c, 0], -1.0, RSG[:, c], ALU.mult, ALU.mult).then_inc(s_nb, 1)

            def h_rows(b):
                dve.wait_ge(s_r2, b + 1)
                v.tensor_scalar(HN[:, b, :], X[:, b, :], MV2[:, 0:1], RS2[:, 0:1],
                                ALU.subtract, ALU.mult).then_inc(s_h, 1)

            def list_tiles():
                dve.wait_ge(s_cnt, 1)
                link(v.tensor_tensor(OVF[:].rearrange("p (k e) -> p k e", e=E),
                                     PS[:, LOGIT, 0:E].unsqueeze(1).to_broadcast([128, MAXE - 1, E]),
                                     THR[:].rearrange("p (k e) -> p k e", e=E), ALU.is_gt))
                link(v.tensor_tensor_scan(PRE[:], OVF[:], ZERO[:, 0:COLS], 0.0, ALU.add, ALU.add))
                link(v.tensor_scalar(LE[:], PRE[:], PM64[:, 0:1], 0.0, ALU.is_le, ALU.add, accum_out=CNT[:, 0:1]))
                link(v.tensor_tensor(CNT[:], CNT[:], PMIN[:], ALU.add))
                link(v.tensor_copy(LST[:, 0:1], CNT[:]))
                v.tensor_scalar(TT[:], PRE[0:1, COLS - 1:COLS], float(E), None, ALU.add)
                v.tensor_scalar(LST[:, 1:2], LST[:, 0:1], E - 1, None, ALU.bitwise_and).then_inc(s_list, 1)

            group_stats(0)
            group_bias(0)
            dve.wait_ge(s_const, 1)
            for i in range(STEPS):
                b, r, k, s = (j if 0 <= j < B else None for j in (i, i - 1, i - 2, i - 3))
                if i in (2, 3):
                    group_bias(i)
                if b is not None:
                    dve.wait_ge(s_zg, b + 1)
                    dve.wait_ge(s_wrc, 2 * (b // 4) + 2)
                    ge(dve, s_wo, b - 1)
                    v.tensor_tensor(ZT[:, b % 2, :, :], ZG[:, b % 2, :, :], WR[:, :, b * S:(b + 1) * S],
                                    ALU.mult).then_inc(s_z, 1)
                if k is not None:
                    dve.wait_ge(s_rk, k + 1)
                    sel = tick(v.tensor_tensor(SEL[:], OH[:, k % 2, :, :],
                                               PS[:, RANK, 0:E].unsqueeze(1).to_broadcast([128, TOPK, E]), ALU.mult))
                    need(sel)
                    link(v.tensor_reduce(RK[:], SEL[:], AX.X, ALU.add))
                    v.scalar_tensor_tensor(SLOT[:, k, :], RK[:], float(E), IDF[:, k % 2, 0:TOPK],
                                           ALU.mult, ALU.add).then_inc(s_slot, 1)
                if i < 3:
                    group_stats(1 + i)
                if r is not None:
                    dve.wait_ge(s_lg, r + 1)
                    v.tensor_reduce(NM[:], PS[:, LOGIT, 0:E], AX.X, ALU.max, negate=True).then_inc(s_nm, 1)
                if b is not None:
                    dve.wait_ge(s_wo, b + 1)
                    v.tensor_tensor(X[:, b, :], PS[:, WO, 0:D], X[:, b, :], ALU.add).then_inc(s_x2, 1)
                if r is not None:
                    dve.wait_ge(s_ex, r + 1)
                    top = tick(v.max(TOP[:], EX[:]))
                if b is not None:
                    dve.wait_ge(s_x2, b + 1)
                    st = tick(v.bn_stats(ST2[:], X[:, b, :]))
                if r is not None:
                    need(top)
                    idx = tick(v.max_index(IDX[:], TOP[:], EX[:]))
                    ts = tick(v.tensor_reduce(TS[:], TOP[:, 0:TOPK], AX.X, ALU.add))
                if b is not None:
                    need(st)
                    mv = tick(v.bn_aggr(MV2[:], ST2[:]))
                if r is not None:
                    need(idx)
                    idf = tick(v.tensor_copy(IDF[:, r % 2, :], IDX[:]))
                    need(ts)
                    td = tick(v.scalar_tensor_tensor(TD[:], ZS[:], TOP_EPS, TS[:], ALU.mult, ALU.add))
                if b is not None:
                    need(mv)
                    v.tensor_scalar(VE2[:], MV2[:, 1:2], LN_EPS, None, ALU.add).then_inc(s_v2, 1)
                if r is not None:
                    need(idf)
                    oh = tick(v.tensor_tensor(OH[:, r % 2, :, :], IOE[:].unsqueeze(1).to_broadcast([128, TOPK, E]),
                                              IDF[:, r % 2, 0:TOPK].unsqueeze(2).to_broadcast([128, TOPK, E]), ALU.is_equal))
                    need(td)
                    rt = tick(v.reciprocal(RT[:], TD[:]))
                    need(oh)
                    ge(dve, s_rk, r - 1)
                    m = tick(v.tensor_reduce(M[:, r % 2, :], OH[:, r % 2, :, :].rearrange("p j e -> p e j"), AX.X, ALU.add))
                    need(rt)
                    v.tensor_scalar(PAY[:, r, :, 1].bitcast(f32), TOP[:, 0:TOPK], RT[:, 0:1], None, ALU.mult)
                    need(m)
                    v.tensor_tensor(MS[:, r + 1, :], MS[:, r, :], M[:, r % 2, :], ALU.add).then_inc(s_m, 1)
                if i == 0:
                    group_bias(1)
                if b is not None and s is None:
                    h_rows(b)
                if s is not None:
                    dve.wait_ge(s_sex, s + 1)
                    ssg = tick(v.scalar_tensor_tensor(SSG[:], SEX[:], 1.0, PS[:, GATE, 0:SF], ALU.add, ALU.mult))
                    if b is not None:
                        h_rows(b)
                    need(ssg)
                    ge(dve, s_st, s)
                    v.scalar_tensor_tensor(SAC[:], SSG[:], 0.5, PS[:, UP, 0:SF], ALU.mult, ALU.mult).then_inc(s_sact, 1)
                if k == B - 1:
                    list_tiles()

            def entries(t, w, col):
                v.tensor_copy(IDR[:, w % U, :], TBL[:, bass.ds(col * 2, 2)] if not isinstance(col, int)
                              else TBL[:, 2 * col:2 * col + 2]).then_inc(s_id, 1)

            def hidden(t, w):
                ge(dve, s_sg, t + (w + 1))
                ge(dve, s_at, t + (w - 1))
                v.scalar_tensor_tensor(AC[:, w % 2, :], SG[:, w % 2, :], IDR[:, w % U, 1:2].bitcast(f32),
                                       PS[:, 2 + w % 2, F:2 * F], ALU.mult, ALU.mult).then_inc(s_act, 1)

            def rows_low(t, w):
                ge(dve, s_xgc, t + (w + 1))
                v.tensor_tensor(XTL[:, w % 2, :, :], PS[:, w % 2, 0:256].rearrange("p (k n) -> p k n", k=KD),
                                XTH[:, w % 2, :, :], ALU.subtract).then_inc(s_xl, 1)

            def weights_low(t, w, k):
                ge(dve, s_wh, t + (w + 1))
                ge(dve, s_gu, t + (w - 1))
                cols = slice(k * SF, (k + 1) * SF)
                v.tensor_tensor(WGL[:, w % 2, cols], WGU[:, (w % R * 2 + k) * SF:(w % R * 2 + k + 1) * SF],
                                WGH[:, w % 2, cols], ALU.subtract).then_inc(s_wl, 1)

            def step(i, u, listed):
                t = i * U
                ge(dve, s_at, t + (u + 1))
                ge(dve, s_d, t + (u - 1))
                v.tensor_copy(ATT[:, u % 2, :, :],
                              PS[0:FC, 4 + u % 2, 0:256].rearrange("p (c n) -> p c n", c=2)).then_inc(s_atc, 1)
                rows_low(t, u + 2)
                weights_low(t, u + 2, 0)
                hidden(t, u + 1)
                weights_low(t, u + 2, 1)
                w = u + LOOK_ID
                ge(dve, s_acc[(w - U) % 2], i * (16 * U // 2) + 16 * ((w - U) // 2 + 1))
                if listed:
                    col = dve.value_load(LROW[0:1, bass.ds(i * (2 * U) + 2 * w, 1)], min_val=0, max_val=BLK * E - 1)
                else:
                    col = t + w
                entries(t, w, col)

            dve.wait_ge(s_tbl, 16)
            for w in range(LOOK_ID):
                entries(0, w, w)
            dve.wait_ge(s_id, LOOK_ID)
            for w in range(2):
                for k in range(KD):
                    weights_low(0, w, k)
            rows_low(0, 0)
            hidden(0, 0)
            rows_low(0, 1)
            dve.wait_ge(s_list, 1)
            T = dve.value_load(TT[0:1, 0:1], min_val=E, max_val=TILES - 1)
            for u in range(U):
                step(0, u, False)
            with dve.Fori(1, E // U - 1) as i:
                for u in range(U):
                    step(i, u, False)
            dve.wait_ge(s_lrow, 16)
            dve.wait_ge(s_tbl_more, 16)
            with dve.Fori(E // U - 1, TILES // U) as i:
                for g in range(0, U, GRP):
                    with dve.If(i * U + g < T):
                        for u in range(g, g + GRP):
                            with dve.If(i * U + u < T):
                                step(i, u, True)
                        dve.sem_inc(s_more[3])

        @block.tensor
        def _(pe):
            mm, tr = nc.tensor.matmul, nc.tensor.transpose
            def x_rows(g):
                pe.wait_ge(s_xn, 2 * g + 2)
                if g >= 2:
                    pe.wait_ge(s_xta, g - 1)
                for k in range(KD):
                    for b in range(2):
                        last = tr(PS[:, X_BANK[g], (k * 2 + b) * 128:(k * 2 + b + 1) * 128],
                                  XN[:, 2 * g + b, k * 128:(k + 1) * 128], IDN)
                last.then_inc(s_xt, 1)

            def warm(n):
                mm(PS[:, 7, 0:n], ZERO[:, 0:128], ZERO[:, 0:n], start=True, stop=True)

            def product(j):
                mm(PS[:, P_BANK[j], :], WW[:, j % 2, :], CT[:, j % 2, (j // 2) * HALF:(j // 2 + 1) * HALF],
                   start=True, stop=True).then_inc(s_p, 1)

            def value(g):
                for h in range(H):
                    for b in range(2):
                        last = mm(PS[:, V_BANK[g], (h * 2 + b) * 128:(h * 2 + b + 1) * 128],
                                  CT[:, h, (2 * g + b) * S:(2 * g + b + 1) * S], WH[:, h, :], start=True, stop=True)
                last.then_inc(s_v, 1)

            def scores(half):
                for h in range(H):
                    for b in range(4 * half, 4 * half + 4):
                        last = mm(PS[:, SCORE[h], 0:S], PT[:, h, b * S:(b + 1) * S],
                                  XNT[:, h, b * S:(b + 1) * S], start=(b == 0), stop=(b == B - 1))
                return last

            def gate(g):
                if g >= 2:
                    pe.wait_ge(s_wrc, g - 1)
                for k in range(KD):
                    last = mm(PS[:, W_BANK[g], :], WGT[:, k, (g % 2) * 128:(g % 2 + 1) * 128],
                              XNT[:, k, (g // 2) * HALF:(g // 2 + 1) * HALF], start=(k == 0), stop=(k == KD - 1))
                last.then_inc(s_wr, 1)

            def attend(g):
                for h in range(H):
                    last = mm(PS[:, 4 + g, :].rearrange("p (b h e) -> p b h e", b=2, h=H)[:, :, h, :], AT[:, h, :],
                              V[:, h, 2 * g:2 * g + 2, :], start=True, stop=True)
                last.then_inc(s_o, 1)

            def z_rows(b):
                pe.wait_ge(s_yn, b + 1)
                ge(pe, s_zg, b)
                for k in range(KD):
                    last = tr(PS[:, ZB, k * 128:(k + 1) * 128], YN[:, b, k * 128:(k + 1) * 128], IDN)
                last.then_inc(s_zt, 1)

            pe.wait_ge(s_init, 2)
            warm(512)
            pe.wait_ge(ld["wh"], 16)
            pe.wait_ge(ld["idn"], 16)
            for h in range(H):
                last = tr(PS[:, 0, h * 128:(h + 1) * 128], WH[:, h, :], IDN)
            last.then_inc(s_wt, 1)
            warm(128)
            pe.wait_ge(s_wtc, 1)
            for h in range(H):
                last = mm(PS[:, 1, h * 128:(h + 1) * 128], WHT[:, h, :], WHT[:, h, :], start=True, stop=True)
            last.then_inc(s_ww, 1)
            pe.wait_ge(ld["ctx0"], 16)
            value(0)
            pe.wait_ge(s_wwc, 1)
            product(0)
            product(1)
            value(1)
            pe.wait_ge(ld["ctx1"], 16)
            product(2)
            product(3)
            x_rows(0)
            x_rows(1)
            x_rows(2)
            x_rows(3)
            pe.wait_ge(s_xta, 2)
            pe.wait_ge(s_pc, 4)
            scores(0)
            pe.wait_ge(s_xtd, 2)
            scores(1).then_inc(s_sc, 1)
            value(2)
            value(3)
            pe.wait_ge(s_a, 1)
            pe.wait_ge(s_vc, 2)
            attend(0)
            pe.wait_ge(ld["wg"], 16)
            pe.wait_ge(s_vc, 3)
            gate(0)
            gate(1)
            z_rows(0)
            attend(1)
            pe.wait_ge(s_vc, 4)
            pe.wait_ge(ld["wo"], 16)
            for i in range(STEPS):
                if 0 <= i - 2 < B:
                    k = i - 2
                    if k == 0:
                        pe.wait_ge(s_const, 1)
                        pe.wait_ge(ld["cst"], 16)
                        pe.wait_ge(s_wrc, 3)
                    pe.wait_ge(s_m, k + 1)
                    ge(pe, s_slot, k)
                    mm(PS[:, RANK, 0:E], TRI, M[:, k % 2, :], start=True, stop=False)
                    mm(PS[:, RANK, 0:E], ONE[:], MS[:, k, :], start=False, stop=True).then_inc(s_rk, 1)
                    if k == B - 1:
                        mm(PS[:, LOGIT, 0:E], ONE[:], MS[:, B, :], start=True, stop=True).then_inc(s_cnt, 1)
                if 0 <= i - 1 < B:
                    r = i - 1
                    pe.wait_ge(s_h, r + 1)
                    ge(pe, s_ex, r)
                    if r == 0:
                        pe.wait_ge(s_yn, 2)
                    for k in range(KD):
                        last = tr(PS[:, LOGIT, 256 + k * 128:256 + (k + 1) * 128], HN[:, r, k * 128:(k + 1) * 128], IDN)
                    last.then_inc(s_ht, 1)
                if 0 <= i - 4 < B:
                    s = i - 4
                    pe.wait_ge(s_sact, s + 1)
                    ge(pe, s_stc, s)
                    if s == 0:
                        pe.wait_ge(s_wrc, 4)
                    for c in range(SF // FC):
                        last = tr(PS[0:FC, STB, c * 128:(c + 1) * 128], SAC[:, c * FC:(c + 1) * FC], IDN)
                    last.then_inc(s_st, 1)
                if i < B:
                    pe.wait_ge(s_z, i + 1)
                    ge(pe, s_x2, i)
                    for k in range(KD):
                        last = mm(PS[:, WO, 0:D], ZT[:, i % 2, k, :], WOT[:, k, :], start=(k == 0), stop=(k == KD - 1))
                    last.then_inc(s_wo, 1)
                if 0 <= i - 1 < B:
                    r = i - 1
                    if r == 0:
                        pe.wait_ge(ld["gw"], 16)
                    pe.wait_ge(s_htc, r + 1)
                    for k in range(KD):
                        last = mm(PS[:, LOGIT, 0:E], HT[:, k, r * S:(r + 1) * S], GWT[:, k, :],
                                  start=(k == 0), stop=(k == KD - 1))
                    last.then_inc(s_lg, 1)
                if i + 1 < B:
                    z_rows(i + 1)
                if i == 0:
                    attend(2)
                    attend(3)
                if 1 <= i < 3:
                    gate(1 + i)
                if 0 <= i - 3 < B:
                    s = i - 3
                    if s == 0:
                        pe.wait_ge(ld["wsg"], 16)
                        pe.wait_ge(s_yn, 6)
                    ge(pe, s_sact, s)
                    for g in range(2):
                        for k in range(KD):
                            last = mm(PS[:, GATE + g, 0:SF], HT[:, k, s * S:(s + 1) * S], WSG[:, k, g * SF:(g + 1) * SF],
                                      start=(k == 0), stop=(k == KD - 1))
                    last.then_inc(s_sgu, 1)
                if 0 <= i - 4 < B:
                    s = i - 4
                    if s == 0:
                        pe.wait_ge(ld["wsd"], 16)
                        pe.wait_ge(s_yn, B)
                    pe.wait_ge(s_stc, s + 1)
                    ge(pe, s_shc, s)
                    for c in range(SF // FC):
                        last = mm(PS[:, SDB, 0:D], SACT[:, c, :], WSD[:, c, :], start=(c == 0), stop=(c == SF // FC - 1))
                    last.then_inc(s_sd, 1)

            def rows(w):
                g = w % XR
                for k in range(KD):
                    last = tr(PS[:, w % 2, k * 128:(k + 1) * 128], XG[:, g, k * 128:(k + 1) * 128], IDN)
                last.then_inc(s_xg, 1)

            def gate_up(t, w):
                for n, (rows_part, weights_part) in enumerate(((XTL, WGH), (XTH, WGH), (XTH, WGL))):
                    for k in range(KD):
                        if n == 2:
                            ge(pe, s_wl, KD * t + (KD * w + k + 1))
                        last = mm(PS[:, 2 + w % 2, 0:SF], rows_part[:, w % 2, k, :],
                                  weights_part[:, w % 2, k * SF:(k + 1) * SF],
                                  start=(n == 0 and k == 0), stop=(n == 2 and k == KD - 1))
                last.then_inc(s_gu, 1)

            def step(i, u):
                t = i * U
                pe.wait_ge(s_act, t + (u + 1))
                ge(pe, s_atc, t + (u - 1))
                for c in range(2):
                    last = tr(PS[0:FC, 4 + u % 2, c * 128:(c + 1) * 128], AC[:, u % 2, c * FC:(c + 1) * FC], IDN)
                last.then_inc(s_at, 1)
                w = u + 1
                pe.wait_ge(s_xl, t + (w + 1))
                pe.wait_ge(s_wh, t + (w + 1))
                pe.wait_ge(s_act, t + w)
                gate_up(t, w)
                pe.wait_ge(s_atc, t + (u + 1))
                ge(pe, s_y, t + (u - 1))
                for c in range(2):
                    last = mm(PS[:, 6 + u % 2, 0:D], ATT[:, u % 2, c, :], WDN[:, u * 2 * D + c * D:u * 2 * D + (c + 1) * D],
                              start=(c == 0), stop=(c == 1))
                last.then_inc(s_d, 1)
                w = u + LOOK_R
                pe.wait_ge(s_g[w % XR], i * (16 * U // XR) + 16 * (w // XR + 1))
                pe.wait_ge(s_xl, t + (w - 1))
                rows(w)

            pe.wait_ge(s_sact, B)
            for f in range(3):
                mm(PS[:, 2, :], ZERO[:, 0:128], ZERO[:], start=True, stop=True)
            pe.wait_ge(s_g[0], 16)
            rows(0)
            pe.wait_ge(s_xl, 1)
            pe.wait_ge(s_wh, 1)
            gate_up(0, 0)
            for w in (1, 2):
                pe.wait_ge(s_g[w], 16)
                rows(w)
            pe.wait_ge(s_list, 1)
            T = pe.value_load(TT[0:1, 0:1], min_val=E, max_val=TILES - 1)
            for u in range(U):
                step(0, u)
            with pe.Fori(1, E // U) as i:
                for u in range(U):
                    step(i, u)
            with pe.Fori(E // U, TILES // U) as i:
                for g in range(0, U, GRP):
                    with pe.If(i * U + g < T):
                        for u in range(g, g + GRP):
                            with pe.If(i * U + u < T):
                                step(i, u)
                        pe.sem_inc(s_more[4])


def shape_constants():
    f = np.float32
    gam = (1.0 - 2.0 ** (-5.0 - np.arange(H, dtype=f))).astype(f)
    idx = np.arange(S, dtype=f)
    expo = idx[None, :] - idx[:, None]
    d = np.where(expo[None] <= 0, gam[:, None, None] ** expo[None], f(0)).astype(f)
    d = (d / np.sqrt(d.sum(axis=-1, dtype=f))[:, None, :]).astype(f)
    mask_t = d.transpose(2, 0, 1).reshape(S, H * S)
    tri = np.triu(np.ones((128, 128), f), 1)
    return np.ascontiguousarray(np.concatenate([np.eye(128, dtype=f), tri, mask_t], axis=1), dtype=f)


def kernel(**inputs):
    import concourse.bacc as bacc
    from concourse.bass_utils import run_bass_kernel_spmd

    a = {k: np.asarray(v) for k, v in inputs.items()}
    chunk = lambda w, p: w.reshape(-1, p, w.shape[-1]).transpose(1, 0, 2)
    arrays = {
        "x": a["x"].transpose(1, 0, 2),
        "ctxT": a["ctx_2048"].reshape(N, H, HD).transpose(2, 1, 0),
        "Wh": a["L0_xattn_Wh"].transpose(1, 0, 2),
        "wg": chunk(a["L0_xattn_wg_w"], 128),
        "wo": chunk(a["L0_xattn_wo_w"], 128),
        "gam": a["L0_xattn_gn_gamma"].reshape(KD, 128).T,
        "bet": a["L0_xattn_gn_beta"].reshape(KD, 128).T,
        "gw": chunk(a["L0_ffn_gate_w"].T, 128),
        "wgu": a["L0_ffn_w_gate_up"].reshape(E, SF, KD, 128).transpose(0, 3, 2, 1).reshape(E, 128, KD * SF),
        "wdn": a["L0_ffn_w_down"].reshape(E, D, 2, FC).transpose(0, 3, 2, 1).reshape(E, FC, 2 * D),
        "wsg": chunk(a["L0_ffn_ws_gate_up"].T, 128),
        "wsd": chunk(a["L0_ffn_ws_down"].T, FC),
        "cst": shape_constants(),
    }
    arrays = {k: np.ascontiguousarray(v) for k, v in arrays.items()}
    nc = bacc.Bacc("TRN2", target_bir_lowering=False, num_devices=1)
    f32 = mybir.dt.float32
    args = [nc.dram_tensor("in_" + k, v.shape, f32, kind="ExternalInput").ap() for k, v in arrays.items()]
    out = nc.dram_tensor("out_rows", (N + 128, D), f32, kind="ExternalOutput").ap()
    program(nc, *args, out)
    r = run_bass_kernel_spmd(nc, [{"in_" + k: v for k, v in arrays.items()}], core_ids=[0])
    return np.asarray(r.results[0]["out_rows"])[:N].reshape(B, S, D)
```
